# Optimizing a Trainium2 kernel written in Bass

```python
import numpy as np
import jax
import jax.numpy as jnp

def _softmax(x, axis=-1):
    return jax.nn.softmax(x, axis=axis)

def _gelu(x):
    return jax.nn.gelu(x, approximate=True)

def _silu(x):
    return jax.nn.silu(x)

def _sigmoid(x):
    return jax.nn.sigmoid(x)

def _layernorm(x, axis=-1, eps=1e-05):
    m = jnp.mean(x, axis=axis, keepdims=True)
    v = jnp.var(x, axis=axis, keepdims=True)
    return (x - m) / jnp.sqrt(v + eps)

def _scatter_add(tgt, idx, src, axis=0):
    return tgt.at[idx].add(src)

def _segment_sum(src, seg, n):
    return jax.ops.segment_sum(src, seg, n)
kernel_name = 'mk_conv_seq_d2_conv_nchw256_r2_3975c7'

def setup_inputs(seed: int=0):
    np.random.seed(seed)
    _w = jnp.asarray

    def _rec_inputs():
        import jax
        import jax.numpy as jnp
        _gk = jax.random.key(seed)
        x = -0.0002928 + 1 * jax.random.normal(jax.random.fold_in(_gk, 1), (4, 128, 32, 32), jnp.float32)
        return x
    x = _rec_inputs()

    def _L0_conv_setup():
        import jax, jax.numpy as jnp
        import numpy as np
        NUM_GROUPS = 8
        EPS = 1e-05

        def _group_norm(x, w, b):
            B, C, H, W = x.shape
            g = NUM_GROUPS
            xg = x.reshape(B, g, C // g, H, W)
            mean = jnp.mean(xg, axis=(2, 3, 4), keepdims=True)
            var = jnp.var(xg, axis=(2, 3, 4), keepdims=True)
            xn = (xg - mean) * jax.lax.rsqrt(var + EPS)
            xn = xn.reshape(B, C, H, W)
            return xn * w[None, :, None, None] + b[None, :, None, None]
        key = jax.random.key(seed)
        ks = jax.random.split(key, 4)
        B, C, H, W = (4, 128, 32, 32)
        x = jax.random.normal(ks[0], (B, C, H, W), dtype=jnp.float32)
        gn_w = jnp.ones((C,), dtype=jnp.float32)
        gn_b = jnp.zeros((C,), dtype=jnp.float32)
        qkv_w = jax.random.normal(ks[1], (3 * C, C), dtype=jnp.float32) * (1.0 / np.sqrt(C))
        qkv_b = jnp.zeros((3 * C,), dtype=jnp.float32)
        proj_w = jax.random.normal(ks[2], (C, C), dtype=jnp.float32) * (1.0 / np.sqrt(C))
        proj_b = jnp.zeros((C,), dtype=jnp.float32)
        return {'x': x, 'gn_w': gn_w, 'gn_b': gn_b, 'qkv_w': qkv_w, 'qkv_b': qkv_b, 'proj_w': proj_w, 'proj_b': proj_b}
    _L0_conv_all = _L0_conv_setup()
    _L0_conv_in = {k: v for k, v in _L0_conv_all.items() if k in ('gn_w', 'gn_b', 'qkv_w', 'qkv_b', 'proj_w', 'proj_b')}
    del _L0_conv_all

    def _L1_conv_setup():
        import jax, jax.numpy as jnp
        import numpy as np
        D_MODEL = 128
        D_STATE = 64
        D_CONV = 4
        HEADDIM = 32
        NHEADS = D_MODEL // HEADDIM
        D_INNER = D_MODEL
        CONV_DIM = D_INNER + 2 * D_STATE
        D_IN_PROJ = 2 * D_INNER + 2 * D_STATE + NHEADS
        EPS = 1e-05

        def _mamba2_core(u, in_w, conv_w, conv_b, dt_bias, A_log, Dp, rms_w, out_w):
            b, L, _ = u.shape
            zxbcdt = jnp.einsum('bld,ed->ble', u, in_w)
            z = zxbcdt[..., :D_INNER]
            xBC = zxbcdt[..., D_INNER:D_INNER + CONV_DIM]
            dt = jax.nn.softplus(zxbcdt[..., -NHEADS:] + dt_bias)
            xc = jax.lax.conv_general_dilated(xBC.transpose(0, 2, 1), conv_w[:, None, :], (1,), [(D_CONV - 1, 0)], dimension_numbers=('NCH', 'OIH', 'NCH'), feature_group_count=CONV_DIM)
            xBC = jax.nn.silu((xc + conv_b[None, :, None]).transpose(0, 2, 1))
            xs = xBC[..., :D_INNER].reshape(b, L, NHEADS, HEADDIM)
            Bm = xBC[..., D_INNER:D_INNER + D_STATE]
            Cm = xBC[..., D_INNER + D_STATE:]
            A = -jnp.exp(A_log)

            def step(state, inp):
                dt_t, x_t, B_t, C_t = inp
                dA = jnp.exp(dt_t * A)
                state = state * dA[:, :, None, None] + (dt_t[:, :, None] * x_t)[..., None] * B_t[:, None, None, :]
                y_t = jnp.einsum('bhpn,bn->bhp', state, C_t)
                return (state, y_t)
            state0 = jnp.zeros((b, NHEADS, HEADDIM, D_STATE), u.dtype)
            _, ys = jax.lax.scan(step, state0, (dt.transpose(1, 0, 2), xs.transpose(1, 0, 2, 3), Bm.transpose(1, 0, 2), Cm.transpose(1, 0, 2)))
            y = ys.transpose(1, 0, 2, 3) + Dp[None, None, :, None] * xs
            y = y.reshape(b, L, D_INNER)
            y = y * jax.nn.silu(z)
            y = y * jax.lax.rsqrt(jnp.mean(y * y, axis=-1, keepdims=True) + EPS) * rms_w
            return jnp.einsum('bld,ed->ble', y, out_w)
        key = jax.random.key(seed)
        ks = jax.random.split(key, 12)
        b, h, w = (4, 32, 32)
        x = jax.random.normal(ks[0], (b, D_MODEL, h, w), jnp.float32)
        s = 0.02
        params = {'norm_g': jnp.ones((D_MODEL,), jnp.float32), 'norm_b': jnp.zeros((D_MODEL,), jnp.float32), 'in_w': jax.random.normal(ks[1], (D_IN_PROJ, D_MODEL), jnp.float32) * s, 'conv_w': jax.random.normal(ks[2], (CONV_DIM, D_CONV), jnp.float32) * 0.1, 'conv_b': jnp.zeros((CONV_DIM,), jnp.float32), 'dt_bias': jax.random.normal(ks[3], (NHEADS,), jnp.float32) * 0.1, 'A_log': jnp.log(jax.random.uniform(ks[4], (NHEADS,), jnp.float32, 1.0, 16.0)), 'Dp': jnp.ones((NHEADS,), jnp.float32), 'rms_w': jnp.ones((D_INNER,), jnp.float32), 'out_w': jax.random.normal(ks[5], (D_MODEL, D_INNER), jnp.float32) * s, 'se1_w': jax.random.normal(ks[6], (D_MODEL // 4, D_MODEL), jnp.float32) * s, 'se1_b': jnp.zeros((D_MODEL // 4,), jnp.float32), 'se2_w': jax.random.normal(ks[7], (D_MODEL, D_MODEL // 4), jnp.float32) * s, 'se2_b': jnp.zeros((D_MODEL,), jnp.float32)}
        return {'x': x, **params}
    _L1_conv_all = _L1_conv_setup()
    _L1_conv_in = {k: v for k, v in _L1_conv_all.items() if k in ('norm_g', 'norm_b', 'in_w', 'conv_w', 'conv_b', 'dt_bias', 'A_log', 'Dp', 'rms_w', 'out_w', 'se1_w', 'se1_b', 'se2_w', 'se2_b')}
    del _L1_conv_all
    return {'x': x, 'L0_conv_gn_w': _L0_conv_in['gn_w'], 'L0_conv_gn_b': _L0_conv_in['gn_b'], 'L0_conv_qkv_w': _L0_conv_in['qkv_w'], 'L0_conv_qkv_b': _L0_conv_in['qkv_b'], 'L0_conv_proj_w': _L0_conv_in['proj_w'], 'L0_conv_proj_b': _L0_conv_in['proj_b'], 'L1_conv_norm_g': _L1_conv_in['norm_g'], 'L1_conv_norm_b': _L1_conv_in['norm_b'], 'L1_conv_in_w': _L1_conv_in['in_w'], 'L1_conv_conv_w': _L1_conv_in['conv_w'], 'L1_conv_conv_b': _L1_conv_in['conv_b'], 'L1_conv_dt_bias': _L1_conv_in['dt_bias'], 'L1_conv_A_log': _L1_conv_in['A_log'], 'L1_conv_Dp': _L1_conv_in['Dp'], 'L1_conv_rms_w': _L1_conv_in['rms_w'], 'L1_conv_out_w': _L1_conv_in['out_w'], 'L1_conv_se1_w': _L1_conv_in['se1_w'], 'L1_conv_se1_b': _L1_conv_in['se1_b'], 'L1_conv_se2_w': _L1_conv_in['se2_w'], 'L1_conv_se2_b': _L1_conv_in['se2_b']}

def reference(x, L0_conv_gn_w, L0_conv_gn_b, L0_conv_qkv_w, L0_conv_qkv_b, L0_conv_proj_w, L0_conv_proj_b, L1_conv_norm_g, L1_conv_norm_b, L1_conv_in_w, L1_conv_conv_w, L1_conv_conv_b, L1_conv_dt_bias, L1_conv_A_log, L1_conv_Dp, L1_conv_rms_w, L1_conv_out_w, L1_conv_se1_w, L1_conv_se1_b, L1_conv_se2_w, L1_conv_se2_b):
    import jax
    import jax.numpy as jnp

    def _L0_conv_ref(x, gn_w, gn_b, qkv_w, qkv_b, proj_w, proj_b):
        import jax, jax.numpy as jnp
        import numpy as np
        NUM_GROUPS = 8
        EPS = 1e-05

        def _group_norm(x, w, b):
            B, C, H, W = x.shape
            g = NUM_GROUPS
            xg = x.reshape(B, g, C // g, H, W)
            mean = jnp.mean(xg, axis=(2, 3, 4), keepdims=True)
            var = jnp.var(xg, axis=(2, 3, 4), keepdims=True)
            xn = (xg - mean) * jax.lax.rsqrt(var + EPS)
            xn = xn.reshape(B, C, H, W)
            return xn * w[None, :, None, None] + b[None, :, None, None]
        B, C, H, W = x.shape
        N = H * W
        h = _group_norm(x, gn_w, gn_b)
        h_flat = h.reshape(B, C, N).transpose(0, 2, 1)
        qkv = jnp.einsum('bnc,oc->bno', h_flat, qkv_w) + qkv_b
        q, k, v = jnp.split(qkv, 3, axis=-1)
        scale = 1.0 / jnp.sqrt(jnp.asarray(C, dtype=x.dtype))
        scores = jnp.einsum('bnc,bmc->bnm', q, k) * scale
        attn = jax.nn.softmax(scores, axis=-1)
        out = jnp.einsum('bnm,bmc->bnc', attn, v)
        out = jnp.einsum('bnc,oc->bno', out, proj_w) + proj_b
        out = out.transpose(0, 2, 1).reshape(B, C, H, W)
        return out + x

    def _L1_conv_ref(x, norm_g, norm_b, in_w, conv_w, conv_b, dt_bias, A_log, Dp, rms_w, out_w, se1_w, se1_b, se2_w, se2_b):
        import jax, jax.numpy as jnp
        import numpy as np
        D_MODEL = 128
        D_STATE = 64
        D_CONV = 4
        HEADDIM = 32
        NHEADS = D_MODEL // HEADDIM
        D_INNER = D_MODEL
        CONV_DIM = D_INNER + 2 * D_STATE
        D_IN_PROJ = 2 * D_INNER + 2 * D_STATE + NHEADS
        EPS = 1e-05

        def _mamba2_core(u, in_w, conv_w, conv_b, dt_bias, A_log, Dp, rms_w, out_w):
            b, L, _ = u.shape
            zxbcdt = jnp.einsum('bld,ed->ble', u, in_w)
            z = zxbcdt[..., :D_INNER]
            xBC = zxbcdt[..., D_INNER:D_INNER + CONV_DIM]
            dt = jax.nn.softplus(zxbcdt[..., -NHEADS:] + dt_bias)
            xc = jax.lax.conv_general_dilated(xBC.transpose(0, 2, 1), conv_w[:, None, :], (1,), [(D_CONV - 1, 0)], dimension_numbers=('NCH', 'OIH', 'NCH'), feature_group_count=CONV_DIM)
            xBC = jax.nn.silu((xc + conv_b[None, :, None]).transpose(0, 2, 1))
            xs = xBC[..., :D_INNER].reshape(b, L, NHEADS, HEADDIM)
            Bm = xBC[..., D_INNER:D_INNER + D_STATE]
            Cm = xBC[..., D_INNER + D_STATE:]
            A = -jnp.exp(A_log)

            def step(state, inp):
                dt_t, x_t, B_t, C_t = inp
                dA = jnp.exp(dt_t * A)
                state = state * dA[:, :, None, None] + (dt_t[:, :, None] * x_t)[..., None] * B_t[:, None, None, :]
                y_t = jnp.einsum('bhpn,bn->bhp', state, C_t)
                return (state, y_t)
            state0 = jnp.zeros((b, NHEADS, HEADDIM, D_STATE), u.dtype)
            _, ys = jax.lax.scan(step, state0, (dt.transpose(1, 0, 2), xs.transpose(1, 0, 2, 3), Bm.transpose(1, 0, 2), Cm.transpose(1, 0, 2)))
            y = ys.transpose(1, 0, 2, 3) + Dp[None, None, :, None] * xs
            y = y.reshape(b, L, D_INNER)
            y = y * jax.nn.silu(z)
            y = y * jax.lax.rsqrt(jnp.mean(y * y, axis=-1, keepdims=True) + EPS) * rms_w
            return jnp.einsum('bld,ed->ble', y, out_w)
        b, c, h, w = x.shape
        L = h * w
        u = x.transpose(0, 2, 3, 1).reshape(b, L, c)
        mu = jnp.mean(u, axis=-1, keepdims=True)
        var = jnp.mean((u - mu) ** 2, axis=-1, keepdims=True)
        u = (u - mu) * jax.lax.rsqrt(var + EPS) * norm_g + norm_b
        out = _mamba2_core(u, in_w, conv_w, conv_b, dt_bias, A_log, Dp, rms_w, out_w)
        out_img = out.reshape(b, h, w, c).transpose(0, 3, 1, 2)
        pooled = jnp.mean(out_img, axis=(2, 3))
        hdn = jax.nn.relu(pooled @ se1_w.T + se1_b)
        attn = jax.nn.sigmoid(hdn @ se2_w.T + se2_b)
        return x + out_img * attn[:, :, None, None]

    def _gn(v, G=32, eps=1e-05):
        B_, C_, H_, W_ = v.shape
        g = v.reshape(B_, G, C_ // G, H_, W_)
        m = jnp.mean(g, axis=(2, 3, 4), keepdims=True)
        s = jnp.var(g, axis=(2, 3, 4), keepdims=True)
        return ((g - m) / jnp.sqrt(s + eps)).reshape(v.shape)

    def _ln_c(v, eps=1e-06):
        m = jnp.mean(v, axis=1, keepdims=True)
        s = jnp.var(v, axis=1, keepdims=True)
        return (v - m) / jnp.sqrt(s + eps)

    def _ln_t(v, eps=1e-05):
        m = jnp.mean(v, axis=-1, keepdims=True)
        s = jnp.var(v, axis=-1, keepdims=True)
        return (v - m) / jnp.sqrt(s + eps)

    def _to_tokens(v):
        B_, C_, H_, W_ = v.shape
        return v.reshape(B_, C_, H_ * W_).transpose(0, 2, 1)

    def _from_tokens(t, like):
        B_, C_, H_, W_ = like.shape
        return t.transpose(0, 2, 1).reshape(B_, C_, H_, W_)
    x = _L0_conv_ref(x, L0_conv_gn_w, L0_conv_gn_b, L0_conv_qkv_w, L0_conv_qkv_b, L0_conv_proj_w, L0_conv_proj_b)
    x = _L1_conv_ref(x, L1_conv_norm_g, L1_conv_norm_b, L1_conv_in_w, L1_conv_conv_w, L1_conv_conv_b, L1_conv_dt_bias, L1_conv_A_log, L1_conv_Dp, L1_conv_rms_w, L1_conv_out_w, L1_conv_se1_w, L1_conv_se1_b, L1_conv_se2_w, L1_conv_se2_b)
    return x

_drawn_inputs = setup_inputs


def setup_inputs(seed=0):
    import zlib

    import numpy as np

    out = dict(_drawn_inputs(seed))
    spreads = {'L0_conv_gn_w': (1.0, 0.2),
     'L0_conv_gn_b': (0.0, 0.1),
     'L0_conv_qkv_b': (0.0, 0.1),
     'L0_conv_proj_b': (0.0, 0.1),
     'L1_conv_norm_g': (1.0, 0.6),
     'L1_conv_norm_b': (0.0, 0.778),
     'L1_conv_conv_b': (0.0, 0.1),
     'L1_conv_Dp': (1.0, 0.6),
     'L1_conv_rms_w': (1.0, 0.6),
     'L1_conv_se1_b': (0.0, 0.8),
     'L1_conv_se2_b': (0.0, 0.8)}
    factors = {'L1_conv_dt_bias': 64.0,
     'L1_conv_A_log': 64.0,
     'L1_conv_se1_w': 41.678,
     'L1_conv_se2_w': 8.0}
    for name, (base, spread) in spreads.items():
        noise = np.random.default_rng([zlib.crc32(name.encode()), seed]).standard_normal(out[name].shape)
        drawn = base * np.exp(spread * noise) if base else spread * noise
        out[name] = jnp.asarray(drawn.astype(out[name].dtype))
    for name, factor in factors.items():
        out[name] = (out[name] * factor).astype(out[name].dtype)
    return out
```

```python
from contextlib import ExitStack

import concourse.bass as bass
from concourse import mybir

F32 = mybir.dt.float32
F32R = mybir.dt.float32r
ALU = mybir.AluOpType
ACT = mybir.ActivationFunctionType
AX = mybir.AxisListType

P = 128
BATCH = 4
TOKENS = 1024
TILES = TOKENS // P
HALF = 512
GROUPS = 8
HEADS = 4
HEADDIM = 32
STATE = 64
TAPS = 4
SE = 32
INPROJ = 2 * P + 2 * STATE + HEADS
EPS = 1e-5
SCORE_SCALE = float(P) ** -0.5
A_LOG_MAX = 88.0
A_SCALE = 2.0 ** -40
DA_LOG_MIN = -200.0


class Signal:

    def __init__(self, sem, per_batch):
        self.sem, self.per_batch = sem, per_batch

    def at(self, t, k):
        return t * self.per_batch + k


def wait(eng, signal, t, k=1, beside=None):
    value = signal.at(t, k)
    if isinstance(value, int):
        if value <= 0:
            return
    eng.wait_ge(signal.sem, value)
    if beside is not None:
        eng.sem_inc(beside, 1)


class Chain:

    def __init__(self, sem, per_batch):
        self.counter, self.k, self.t = Signal(sem, per_batch), 0, 0

    def start(self, t):
        self.k, self.t = 0, t

    def link(self, eng, instruction):
        self.k += 1
        instruction.then_inc(self.counter.sem, 1)
        wait(eng, self.counter, self.t, self.k)

    def end(self):
        assert self.k == self.counter.per_batch, (self.k, self.counter.per_batch)


SCORE_USES = ["q"] + [f"S{i}" for i in range(TILES)]
TURN_USES = (["V0", "V1"] + [f"T{i}{h}" for i in range(5) for h in "ab"] + ["invT", "invB"]
             + [f"T{i}{h}" for i in range(5, 8) for h in "ab"] + ["invT1", "invB1"])
MAMBA_USES = (["xT0", "xT1", "rT", "rB0", "rB1", "inx0", "inx1", "dt", "inbc0", "inbc1", "inz0", "inz1",
               "dAT", "cd0", "cd1", "xsT0", "xsT1", "BT"]
              + [f"Lb{c}" for c in range(TILES)]
              + ["U", "G0", "G1", "ST0", "ST1", "Yo0", "Yo1", "Y0", "Y1", "ss", "yrT", "yrB0", "yrB1",
                 "out0", "out1", "se1", "se2"])


def placed(uses, banks):
    where, count = {}, [0] * banks
    for n, name in enumerate(uses):
        bank = n % banks
        count[bank] += 1
        where[name] = (bank, count[bank])
    return where, count


def build(nc, x, gn_w, gn_b, qkv_w, qkv_b, proj_w, proj_b, norm_g, norm_b, in_w, conv_w, conv_b, dt_bias,
          A_log, Dp, rms_w, out_w, se1_w, se1_b, se2_w, se2_b, out):
    x_d = x.rearrange("b c h w -> b c (h w)")
    out_d = out.rearrange("b c h w -> b c (h w)")
    turn_at, turn_n = placed(TURN_USES, 2)
    mamba_at, mamba_n = placed(MAMBA_USES, 3)

    with ExitStack() as ctx:
        def sb(name, shape, dt=F32):
            return ctx.enter_context(nc.sbuf_tensor(name, shape, dt))

        def signal(name, per_batch=1):
            return Signal(ctx.enter_context(nc.semaphore(name)), per_batch)

        scores = ctx.enter_context(nc.psum_tensor("scores", [P, TOKENS], F32))
        turn = [ctx.enter_context(nc.psum_tensor(f"turn{b}", [P, HALF], F32)) for b in range(2)]
        attn_out = ctx.enter_context(nc.psum_tensor("attn_out", [P, HALF], F32))
        mb = [ctx.enter_context(nc.psum_tensor(f"mamba{b}", [P, HALF], F32)) for b in range(3)]

        ident = sb("ident", [P, P])
        ident4 = sb("ident4", [P, HEADS, P])
        center = sb("center", [P, P])
        group_avg = sb("group_avg", [P, P])
        zeros = sb("zeros", [P, P])
        ones = sb("ones", [P, 1])
        past_first = sb("past_first", [2 * 32, P])
        neg_half = sb("neg_half", [P, TILES])
        pick_row = sb("pick_row", [2 * 32, 32], F32R)
        pick_head = sb("pick_head", [2 * 32, TILES, P], F32R)

        x_all = sb("x_all", [P, BATCH * TOKENS])
        wqkv = sb("wqkv", [P, 3, P])
        wp = sb("wp", [P, P])
        win = sb("win", [P, 4, P])
        wout = sb("wout", [P, P])
        wse1 = sb("wse1", [SE, P])
        wse2 = sb("wse2", [P, SE])
        (GNW, GNB, QB, VB, PB, NG, NB, RMSW, DP, SE2B, QA, OB, BZ, BX, BBC) = range(15)
        col = sb("col", [P, 15])
        se1b = sb("se1b", [SE, 1])
        conv = sb("conv", [P, 2, TAPS + 1])
        dtb_in = sb("dtb_in", [P, HEADS])
        alog = sb("alog", [P, HEADS])

        key_query_hi = sb("key_query_hi", [P, P], F32R)
        key_query_lo = sb("key_query_lo", [P, P], F32R)
        wpT = sb("wpT", [P, P])
        value_proj_hi = sb("value_proj_hi", [P, P], F32R)
        value_proj_lo = sb("value_proj_lo", [P, P], F32R)
        winT = sb("winT", [P, INPROJ])
        winTg = sb("winTg", [P, INPROJ])
        winC = sb("winC", [P, INPROJ])
        woutT = sb("woutT", [P, P])
        se1T = sb("se1T", [P, SE])
        se2T = sb("se2T", [SE, P])
        dtb = sb("dtb", [P, HEADS])
        a_exp = sb("a_exp", [P, HEADS])
        a_neg = sb("a_neg", [P, HEADS])
        half_bz = sb("half_bz", [P, 1])
        half_se2b = sb("half_se2b", [P, 1])

        gn_raw = sb("gn_raw", [P, BATCH, 2, 6])
        gn_mv = sb("gn_mv", [P, BATCH, 2])
        gn_mean = sb("gn_mean", [P, BATCH])
        gn_dev = sb("gn_dev", [P, BATCH])
        gn_ve = sb("gn_ve", [P, BATCH])
        gn_rstd = sb("gn_rstd", [P, BATCH])
        gn_scale = sb("gn_scale", [P, BATCH])
        gn_bias = sb("gn_bias", [P, BATCH])

        h32 = sb("h32", [P, TOKENS])
        h_hi = sb("h_hi", [P, TOKENS], F32R)
        h_lo = sb("h_lo", [P, TOKENS], F32R)
        q_hi = sb("q_hi", [P, TOKENS], F32R)
        q_lo = sb("q_lo", [P, TOKENS], F32R)
        v_hi = sb("v_hi", [P, TILES, P], F32R)
        v_lo = sb("v_lo", [P, TILES, P], F32R)
        neg_max = sb("neg_max", [P, TILES])
        row_sum = sb("row_sum", [P, TILES])
        probs = sb("probs", [P, 2, TOKENS])
        pT_hi = sb("pT_hi", [P, 2, TILES, 2 * P], F32R)
        pT_lo = sb("pT_lo", [P, 2, TILES, 2 * P], F32R)
        inv = sb("inv", [P, TILES])
        inv_rows = sb("inv_rows", [P, 2, 32])
        inv_T = sb("inv_T", [2 * 32, P], F32R)
        inv_b = sb("inv_b", [P, HALF])
        x1 = sb("x1", [P, TOKENS])

        x1res = sb("x1res", [P, TOKENS])
        ln_raw = sb("ln_raw", [P, TILES, 6])
        ln_mv = sb("ln_mv", [P, TILES, 2])
        ln_ve = sb("ln_ve", [P, TILES])
        ln_rstd = sb("ln_rstd", [P, TILES])
        ln_rows = sb("ln_rows", [P, 2, 32])
        ln_T = sb("ln_T", [2 * 32, P], F32R)
        u = sb("u", [P, TOKENS])
        PAD = TAPS - 1
        raw = sb("raw", [P, 2, PAD + TOKENS])
        pre = sb("pre", [P, 2, TOKENS])
        th = sb("th", [P, 2, TOKENS])
        xs = sb("xs", [P, TOKENS])
        B = sb("B", [STATE, TOKENS])
        C = sb("C", [STATE, TOKENS])
        thz = sb("thz", [P, TOKENS])
        zv = sb("zv", [P, TOKENS])
        gate = sb("gate", [P, TOKENS])
        N32 = TILES * HEADS
        dtx = sb("dtx", [P, N32])
        dta = sb("dta", [P, N32])
        dte = sb("dte", [P, N32])
        dtw = sb("dtw", [P, 6, N32])
        dt = sb("dt", [P, N32])
        dA = sb("dA", [P, N32])
        dA_rows = sb("dA_rows", [P, 2, 32])
        dA_T = sb("dA_T", [2 * 32, P], F32R)
        dA_Tz = sb("dA_Tz", [2 * 32, P], F32R)
        decay_in = sb("decay_in", [P, TOKENS])
        xdt = sb("xdt", [P, N32, HEADDIM])
        xend = u[:, :].rearrange("p (a b) -> p a b", b=HEADDIM)
        BT = sb("BT", [P, TILES, STATE])
        L = sb("L", [P, N32, P])
        M = L
        state = sb("state", [P, TILES, STATE])
        stateT = sb("stateT", [STATE, TILES, P])
        yo, y = pre[:, 0, :], pre[:, 1, :]
        sq, y_b = th[:, 0, :], th[:, 1, :]
        y2 = xs
        ms = sb("ms", [P, TILES])
        y_rstd = sb("y_rstd", [P, TILES])
        y_rows = sb("y_rows", [P, 2, 32])
        y_T = sb("y_T", [2 * 32, P], F32R)
        o_img = decay_in
        pooled = sb("pooled", [P, 2])
        hdn = sb("hdn", [SE, 1])
        tha = sb("tha", [P, 1])
        att = sb("att", [P, 1])
        fin = o_img

        x_in = [signal(f"x_in{b}") for b in range(BATCH)]
        attn_w_in = signal("attn_w_in")
        mamba_w_in = signal("mamba_w_in")
        consts_done = signal("consts_done")
        pool_step = signal("pool_step")
        gn_step = signal("gn_step")
        gn_mm = signal("gn_mm")
        gn_pow = signal("gn_pow")
        gn_ready = signal("gn_ready")
        prep_mm = signal("prep_mm")
        prep_evac = signal("prep_evac")
        dve_prep = signal("dve_prep")
        alog_clamped, a_exp_ready = signal("alog_clamped"), signal("a_exp_ready")
        scores_filled = signal("scores_filled", len(SCORE_USES))
        pe_passed, dve_passed, pool_passed = (ctx.enter_context(nc.semaphore(n))
                                              for n in ("pe_passed", "dve_passed", "pool_passed"))
        turn_filled = [signal(f"turn_filled{b}", turn_n[b]) for b in range(2)]
        h_ready = signal("h_ready")
        h_split = signal("h_split", 2)
        q_hi_ready, q_lo_ready = signal("q_hi_ready", 2), signal("q_lo_ready", 2)
        v_hi_ready, v_lo_ready = signal("v_hi_ready", 2), signal("v_lo_ready", 2)
        max_ready = signal("max_ready", TILES)
        exp_done = signal("exp_done", TILES)
        pT_hi_ready, pT_lo_ready = signal("pT_hi_ready", 2 * TILES), signal("pT_lo_ready", 2 * TILES)
        out_taken = signal("out_taken", 2)
        pv_done = signal("pv_done", 4)
        inv_rows_ready = signal("inv_rows_ready", 2)
        inv_T_ready = signal("inv_T_ready", 2)
        inv_b_ready = signal("inv_b_ready", 2)
        x1_ready = signal("x1_ready", 2)
        attn_dve = Chain(ctx.enter_context(nc.semaphore("attn_dve")), 4)
        mb_filled = [signal(f"mb_filled{b}", mamba_n[b]) for b in range(3)]
        x1res_ready = signal("x1res_ready")
        ln_stats = signal("ln_stats", 2)
        ln_ve_ready, ln_rstd_ready = signal("ln_ve_ready"), signal("ln_rstd_ready")
        ln_rows_ready, ln_T_ready = signal("ln_rows_ready"), signal("ln_T_ready")
        u_ready = signal("u_ready", 2)
        raw_ready = signal("raw_ready", 4)
        pre_ready = signal("pre_ready", 2)
        th_ready = signal("th_ready", 2)
        xs_ready, bc_ready = signal("xs_ready"), signal("bc_ready")
        z_ready, gate_ready = signal("z_ready", 4), signal("gate_ready")
        gate_step = signal("gate_step")
        dtx_ready = signal("dtx_ready")
        dta_ready, dte_ready = signal("dta_ready"), signal("dte_ready")
        da_log_ready, dA_ready = signal("da_log_ready"), signal("dA_ready")
        dA_rows_ready, dA_T_ready = signal("dA_rows_ready"), signal("dA_T_ready", 2)
        decay_ready, L_ready = signal("decay_ready", TILES), signal("L_ready", TILES)
        BT_ready = signal("BT_ready")
        xdt_ready, xend_ready = signal("xdt_ready", 2), signal("xend_ready")
        M_ready = signal("M_ready", TILES)
        state_ready, stateT_ready = signal("state_ready", TILES - 1), signal("stateT_ready", 2)
        yo_ready, y_ready = signal("yo_ready", 2), signal("y_ready", 2)
        y2_ready, sq_ready = signal("y2_ready"), signal("sq_ready")
        ms_ready, y_rstd_ready = signal("ms_ready"), signal("y_rstd_ready")
        y_rows_ready, y_T_ready = signal("y_rows_ready"), signal("y_T_ready")
        y_b_ready = signal("y_b_ready", 2)
        pooled_ready, hdn_ready, tha_ready = signal("pooled_ready", 2), signal("hdn_ready"), signal("tha_ready")
        fin_ready = signal("fin_ready")
        out_sent = signal("out_sent", 16)
        mamba_dve = Chain(ctx.enter_context(nc.semaphore("mamba_dve")), 27)

        scores_read = {"q": (q_lo_ready, 2)} | {f"S{i}": (exp_done, i + 1) for i in range(TILES)}
        turn_read = {"V0": (v_lo_ready, 1), "V1": (v_lo_ready, 2), "invT": (inv_T_ready, 1),
                     "invB": (inv_b_ready, 1), "invT1": (inv_T_ready, 2), "invB1": (inv_b_ready, 2)}
        for i in range(TILES):
            turn_read |= {f"T{i}a": (pT_lo_ready, 2 * i + 1), f"T{i}b": (pT_lo_ready, 2 * i + 2)}
        mamba_read = {"xT0": (ln_stats, 1), "xT1": (ln_stats, 2), "rT": (ln_T_ready, 1),
                      "rB0": (u_ready, 1), "rB1": (u_ready, 2), "inx0": (raw_ready, 1),
                      "inx1": (raw_ready, 2), "dt": (dtx_ready, 1), "inbc0": (raw_ready, 3),
                      "inbc1": (raw_ready, 4), "inz0": (z_ready, 2), "inz1": (z_ready, 4),
                      "dAT": (dA_T_ready, 2), "cd0": (decay_ready, 4), "cd1": (decay_ready, 8),
                      "xsT0": (xdt_ready, 1), "xsT1": (xdt_ready, 2), "BT": (BT_ready, 1),
                      "G0": (M_ready, 4), "G1": (M_ready, 8), "U": (state_ready, 7),
                      "ST0": (stateT_ready, 1), "ST1": (stateT_ready, 2), "Yo0": (yo_ready, 1),
                      "Yo1": (yo_ready, 2), "Y0": (y_ready, 1), "Y1": (y_ready, 2), "ss": (ms_ready, 1),
                      "yrT": (y_T_ready, 1), "yrB0": (y_b_ready, 1), "yrB1": (y_b_ready, 2),
                      "out0": (pooled_ready, 1), "out1": (pooled_ready, 2), "se1": (hdn_ready, 1),
                      "se2": (tha_ready, 1)}
        mamba_read |= {f"Lb{c}": (L_ready, c + 1) for c in range(TILES)}

        def bank_free(pe, t, uses, banks, read, name, beside=None):
            n = uses.index(name)
            if n >= banks:
                signal, k = read[uses[n - banks]]
                wait(pe, signal, t, k, beside)
            else:
                last = max(m for m in range(len(uses)) if m % banks == n)
                signal, k = read[uses[last]]
                wait(pe, signal, t - 1, k, beside)

        def turn_fill(pe, t, name, beside=None):
            bank_free(pe, t, TURN_USES, 2, turn_read, name, beside)
            return turn[turn_at[name][0]], turn_filled[turn_at[name][0]].sem

        def turn_take(eng, t, name):
            bank, nth = turn_at[name]
            wait(eng, turn_filled[bank], t, nth)
            return turn[bank]

        def mamba_fill(pe, t, name, beside=None):
            bank_free(pe, t, MAMBA_USES, 3, mamba_read, name, beside)
            return mb[mamba_at[name][0]], mb_filled[mamba_at[name][0]].sem

        def mamba_take(eng, t, name):
            bank, nth = mamba_at[name]
            wait(eng, mb_filled[bank], t, nth)
            return mb[bank]

        def mamba_filled(eng, t, name):
            bank, nth = mamba_at[name]
            wait(eng, mb_filled[bank], t, nth)

        STEPS = [["x1T"], ["ln_rows", "ln_bcast"], ["in_x", "dt_in", "in_bc"], ["in_z", "conv_x", "dt"],
                 ["xs", "dA_rows", "conv_bc"], ["decay", "xsT", "BT"],
                 ["L0", "L1", "L2", "L3"], ["L4", "L5", "L6", "L7", "U", "G0", "G1"],
                 ["stateT", "Y", "square", "y_rows"], ["out", "se", "fin"]]
        SLOTS = len(STEPS)

        def run_streams(eng, attention, mamba, between):
            for slot in range(SLOTS):
                attention(0, slot)
                between(slot)

            def both(t):
                for slot in range(SLOTS):
                    attention(t, slot)
                    for step in STEPS[slot]:
                        mamba(t - 1, step)

            both(1)
            with eng.Fori(2, BATCH) as t:
                both(t)
            for slot in range(SLOTS):
                for step in STEPS[slot]:
                    mamba(BATCH - 1, step)

        block = ctx.enter_context(nc.Block())

        @block.sync
        def _(sp):
            sp.dma_start(x_all[:, 0:TOKENS], x_d[0]).then_inc(x_in[0].sem, 16)
            sp.dma_start(wqkv[:, :, :], qkv_w.rearrange("(k o) c -> o k c", k=3)).then_inc(attn_w_in.sem, 16)
            sp.dma_start(wp[:, :], proj_w).then_inc(attn_w_in.sem, 16)
            for b in range(1, BATCH):
                sp.dma_start(x_all[:, b * TOKENS:(b + 1) * TOKENS], x_d[b]).then_inc(x_in[b].sem, 16)
            for k in range(3):
                sp.dma_start(win[:, k, :], in_w[k * P:(k + 1) * P, :]).then_inc(mamba_w_in.sem, 16)
            sp.dma_start(win[0:HEADS, 3, :], in_w[3 * P:INPROJ, :]).then_inc(mamba_w_in.sem, 16)
            sp.dma_start(wout[:, :], out_w).then_inc(mamba_w_in.sem, 16)
            sp.dma_start(wse1[:, :], se1_w).then_inc(mamba_w_in.sem, 16)
            sp.dma_start(wse2[:, :], se2_w).then_inc(mamba_w_in.sem, 16)

            def store(t):
                wait(sp, fin_ready, t)
                sp.dma_start(out_d[bass.ds(t, 1)].rearrange("b c n -> (b c) n"), fin[:, :]).then_inc(out_sent.sem, 16)

            with sp.Fori(0, BATCH) as t:
                store(t)
            sp.wait_ge(out_sent.sem, 16 * BATCH)

        @block.gpsimd
        def _(pool):
            pool.memset(ident[:, :], 0.0).then_inc(pool_step.sem, 1)
            pool.memset(group_avg[:, :], 1.0 / (P // GROUPS)).then_inc(pool_step.sem, 1)
            pool.wait_ge(pool_step.sem, 2)
            pool.affine_select(out=ident[:, :], in_=ident[:, :], compare_op=ALU.not_equal, fill=1.0, base=0,
                               pattern=[[-1, P]], channel_multiplier=1).then_inc(consts_done.sem, 1)
            width = P // GROUPS
            view = group_avg[:, :].rearrange("p (g r) -> p g r", g=GROUPS)
            pool.affine_select(out=view, in_=view, compare_op=ALU.is_ge, fill=0.0, base=0,
                               pattern=[[-width, GROUPS], [0, width]], channel_multiplier=1
                               ).then_inc(pool_step.sem, 1)
            pool.wait_ge(pool_step.sem, 3)
            pool.affine_select(out=view, in_=view, compare_op=ALU.is_ge, fill=0.0, base=width - 1,
                               pattern=[[width, GROUPS], [0, width]], channel_multiplier=-1
                               ).then_inc(consts_done.sem, 1)
            pool.memset(zeros[:, :], 0.0).then_inc(consts_done.sem, 1)
            pool.memset(ones[:, :], 1.0).then_inc(consts_done.sem, 1)
            pool.memset(past_first[:, 1:P], 1.0).then_inc(consts_done.sem, 1)
            pool.memset(past_first[:, 0:1], 0.0).then_inc(consts_done.sem, 1)
            pool.memset(neg_half[:, :], -0.5).then_inc(consts_done.sem, 1)
            pool.memset(inv_rows[:, :, :], 0.0).then_inc(consts_done.sem, 1)
            pool.memset(ln_rows[:, :, :], 0.0).then_inc(consts_done.sem, 1)
            pool.memset(y_rows[:, :, :], 0.0).then_inc(consts_done.sem, 1)
            pool.memset(raw[:, :, 0:PAD], 0.0).then_inc(consts_done.sem, 1)
            pool.wait_ge(consts_done.sem, 7)
            for n, (b0, b1) in enumerate(((0, 1), (1, BATCH))):
                pool.wait_ge(gn_step.sem, 3 * n + 3)
                pool.tensor_tensor(gn_rstd[:, b0:b1], gn_ve[:, b0:b1], neg_half[:, b0:b1], ALU.pow
                                   ).then_inc(gn_pow.sem, 1)

            def mamba(t):
                wait(pool, x1_ready, t, 2)
                wait(pool, fin_ready, t - 1, beside=pool_passed)
                pool.tensor_copy(x1res[:, :], x1[:, :]).then_inc(x1res_ready.sem, 1)
                wait(pool, ln_ve_ready, t)
                wait(pool, ln_rows_ready, t - 1)
                pool.tensor_tensor(ln_rstd[:, :], ln_ve[:, :], neg_half[:, :], ALU.pow
                                   ).then_inc(ln_rstd_ready.sem, 1)
                wait(pool, z_ready, t, 4)
                wait(pool, y2_ready, t - 1)
                pool.tensor_tensor(gate[:, :], thz[:, :], zv[:, :], ALU.mult).then_inc(gate_step.sem, 1)
                wait(pool, gate_step, t)
                pool.tensor_tensor(gate[:, :], gate[:, :], zv[:, :], ALU.add).then_inc(gate_ready.sem, 1)
                wait(pool, ms_ready, t)
                wait(pool, y_rows_ready, t - 1)
                pool.tensor_tensor(y_rstd[:, :], ms[:, :], neg_half[:, :], ALU.pow
                                   ).then_inc(y_rstd_ready.sem, 1)

            mamba(0)
            with pool.Fori(1, BATCH) as t:
                mamba(t)

        @block.scalar
        def _(act):
            vectors = ((GNW, gn_w), (GNB, gn_b), (QB, qkv_b[0:P]), (VB, qkv_b[2 * P:3 * P]), (PB, proj_b))
            for c, v in vectors:
                act.dma_start(col[:, c:c + 1], v.rearrange("(p a) -> p a", a=1)).then_inc(attn_w_in.sem, 16)
            for c, v in ((NG, norm_g), (NB, norm_b), (RMSW, rms_w), (SE2B, se2_b)):
                act.dma_start(col[:, c:c + 1], v.rearrange("(p a) -> p a", a=1)).then_inc(mamba_w_in.sem, 16)
            act.dma_start(col[:, DP:DP + 1],
                          Dp.rearrange("(h a) -> h a", a=1).broadcast_to([HEADS, HEADDIM])
                          ).then_inc(mamba_w_in.sem, 16)
            act.dma_start(se1b[:, :], se1_b.rearrange("(p a) -> p a", a=1)).then_inc(mamba_w_in.sem, 16)
            for k in range(2):
                act.dma_start(conv[:, k, 0:TAPS], conv_w[k * P:(k + 1) * P, :]).then_inc(mamba_w_in.sem, 16)
                act.dma_start(conv[:, k, TAPS:TAPS + 1],
                              conv_b[k * P:(k + 1) * P].rearrange("(p a) -> p a", a=1)
                              ).then_inc(mamba_w_in.sem, 16)
            act.dma_start(dtb_in[:, :], dt_bias.rearrange("(a h) -> a h", a=1).broadcast_to([P, HEADS])
                          ).then_inc(mamba_w_in.sem, 16)
            act.dma_start(alog[:, :], A_log.rearrange("(a h) -> a h", a=1).broadcast_to([P, HEADS])
                          ).then_inc(mamba_w_in.sem, 16)

            def attn_setup(t):
                act.wait_ge(gn_ready.sem, 1 if isinstance(t, int) and t == 0 else 2)
                wait(act, h_split, t - 1, 2)
                act.activation(h32[:, :], x_all[:, bass.ds(t * TOKENS, TOKENS)], ACT.Identity,
                               bias=gn_bias[:, bass.ds(t, 1)], scale=gn_scale[:, bass.ds(t, 1)]
                               ).then_inc(h_ready.sem, 1)
                wait(act, scores_filled, t, 1)
                for n in range(2):
                    half = slice(n * HALF, (n + 1) * HALF)
                    act.activation(q_hi[:, half], scores[:, half], ACT.Identity, bias=col[:, QA:QA + 1]
                                   ).then_inc(q_hi_ready.sem, 1)
                for n in range(2):
                    bank = turn_take(act, t, f"V{n}")
                    act.activation(v_hi[:, 4 * n:4 * n + 4, :], bank[:, :].rearrange("p (a b) -> p a b", a=4),
                                   ACT.Copy).then_inc(v_hi_ready.sem, 1)

            def attn_turned(t, i):
                g, i2 = divmod(i, 2)
                if i2 == 0:
                    wait(act, pv_done, t, g - 1)
                for n in range(2):
                    bank = turn_take(act, t, f"T{i}{'ab'[n]}")
                    act.activation(pT_hi[:, g % 2, 4 * n:4 * n + 4, i2 * P:(i2 + 1) * P],
                                   bank[:, :].rearrange("p (a b) -> p a b", a=4), ACT.Copy
                                   ).then_inc(pT_hi_ready.sem, 1)

            def attn_exp(t, i):
                wait(act, max_ready, t, i + 1)
                wait(act, turn_filled[1], t, turn_at[f"T{i - 2}b"][1]) if i >= 2 else \
                    wait(act, turn_filled[1], t - 1, turn_at[f"T{i + 6}b"][1])
                if i % 4 == 0:
                    wait(act, inv_rows_ready, t - 1, i // 4 + 1)
                act.activation(probs[:, i % 2, :], scores[:, :], ACT.Exp, bias=neg_max[:, i:i + 1],
                               accum_out=row_sum[:, i:i + 1]).then_inc(exp_done.sem, 1)

            def attn_norm(t, h):
                bank = turn_take(act, t, "invB" if h == 0 else "invB1")
                wait(act, x1_ready, t, h)
                act.activation(inv_b[:, :], bank[:, :], ACT.Copy).then_inc(inv_b_ready.sem, 1)

            def attention(t, slot):
                if slot == 0:
                    attn_setup(t)
                if slot == 6:
                    attn_norm(t, 0)
                if 1 <= slot <= 8:
                    attn_turned(t, slot - 1)
                if slot < TILES:
                    attn_exp(t, slot)
                if slot == 8:
                    attn_norm(t, 1)

            def mamba(t, step):
                if step == "in_x" or step == "in_bc":
                    k, name, bias = (0, "inx", BX) if step == "in_x" else (1, "inbc", BBC)
                    wait(act, pre_ready, t - 1, k + 1)
                    for n in range(2):
                        bank = mamba_take(act, t, f"{name}{n}")
                        act.activation(raw[:, k, PAD + n * HALF:PAD + (n + 1) * HALF], bank[:, :],
                                       ACT.Identity, bias=col[:, bias:bias + 1]).then_inc(raw_ready.sem, 1)
                elif step == "in_z":
                    wait(act, gate_ready, t - 1)
                    for n in range(2):
                        half = slice(n * HALF, (n + 1) * HALF)
                        bank = mamba_take(act, t, f"inz{n}")
                        act.activation(thz[:, half], bank[:, :], ACT.Tanh, bias=half_bz[:, :], scale=0.5
                                       ).then_inc(z_ready.sem, 1)
                        act.activation(zv[:, half], bank[:, :], ACT.Identity, bias=half_bz[:, :], scale=0.5
                                       ).then_inc(z_ready.sem, 1)
                elif step == "dt":
                    wait(act, dta_ready, t)
                    act.activation(dte[:, :], dta[:, :], ACT.Exp, scale=-1.0).then_inc(dte_ready.sem, 1)
                elif step == "xs":
                    wait(act, pre_ready, t, 1)
                    act.activation(th[:, 0, :], pre[:, 0, :], ACT.Tanh).then_inc(th_ready.sem, 1)
                elif step == "dA_rows":
                    wait(act, da_log_ready, t)
                    act.activation(dA[:, :], dtw[:, 4, :], ACT.Exp, scale=1.0 / A_SCALE
                                   ).then_inc(dA_ready.sem, 1)
                elif step == "conv_bc":
                    wait(act, pre_ready, t, 2)
                    act.activation(th[:, 1, :], pre[:, 1, :], ACT.Tanh).then_inc(th_ready.sem, 1)
                elif step == "BT":
                    mamba_filled(act, t - 1, "U")
                    bank = mamba_take(act, t, "BT")
                    act.activation(BT[:, :, :], bank[:, :].rearrange("p (c n) -> p c n", c=TILES), ACT.Copy
                                   ).then_inc(BT_ready.sem, 1)
                elif step == "stateT":
                    mamba_filled(act, t - 1, "Yo1")
                    bank = mamba_take(act, t, "ST0")
                    act.activation(stateT[:, 1:4, :], bank[0:STATE, P:4 * P].rearrange("p (c n) -> p c n", c=3),
                                   ACT.Copy).then_inc(stateT_ready.sem, 1)
                    bank = mamba_take(act, t, "ST1")
                    act.activation(stateT[:, 4:8, :], bank[0:STATE, :].rearrange("p (c n) -> p c n", c=4),
                                   ACT.Copy).then_inc(stateT_ready.sem, 1)
                elif step == "square":
                    mamba_filled(act, t - 1, "ss")
                    wait(act, y2_ready, t)
                    act.activation(sq[:, :], y2[:, :], ACT.Square).then_inc(sq_ready.sem, 1)
                elif step == "out":
                    wait(act, pooled_ready, t - 1, 2)
                    for n in range(2):
                        bank = mamba_take(act, t, f"yrB{n}")
                        act.activation(y_b[:, n * HALF:(n + 1) * HALF], bank[:, :], ACT.Copy
                                       ).then_inc(y_b_ready.sem, 1)
                elif step == "se":
                    bank = mamba_take(act, t, "se1")
                    act.activation(hdn[:, :], bank[0:SE, 0:1], ACT.Relu, bias=se1b[:, :], scale=1.0 / TOKENS
                                   ).then_inc(hdn_ready.sem, 1)
                    bank = mamba_take(act, t, "se2")
                    act.activation(tha[:, :], bank[:, 0:1], ACT.Tanh, bias=half_se2b[:, :], scale=0.5
                                   ).then_inc(tha_ready.sem, 1)

            def prepare(slot):
                if slot == 2:
                    act.wait_ge(alog_clamped.sem, 1)
                    act.activation(a_exp[:, :], alog[:, :], ACT.Exp).then_inc(a_exp_ready.sem, 1)

            run_streams(act, attention, mamba, prepare)

        @block.vector
        def _(dve):
            V = nc.vector
            prep = [0]

            def step_done(ins):
                prep[0] += 1
                ins.then_inc(dve_prep.sem, 1)
                dve.wait_ge(dve_prep.sem, prep[0])

            dve.wait_ge(consts_done.sem, 11)
            for h in range(HEADS):
                V.tensor_copy(ident4[:, h, :], ident[:, :])
            V.tensor_scalar(center[:, :], ident[:, :], 1.0 / P, None, ALU.subtract)
            step_done(V.tensor_tensor(pick_row[:, :], ident[0:64, 0:32], ident[0:64, 32:64], ALU.add))
            step_done(V.tensor_copy(
                pick_head[:, :, :].rearrange("k c (h p) -> k (c h) p", h=HEADS),
                pick_row[:, :].bitcast(F32).unsqueeze(2).broadcast_to([64, 32, HEADDIM])))

            def group_norm(n, b0, b1):
                for b in range(b0, b1):
                    dve.wait_ge(x_in[b].sem, 16)
                    for k in range(2):
                        ins = V.bn_stats(gn_raw[:, b, k, :], x_all[:, b * TOKENS + k * HALF:b * TOKENS + (k + 1) * HALF])
                step_done(ins)
                for b in range(b0, b1):
                    ins = V.bn_aggr(gn_mv[:, b, :], gn_raw[:, b, :, :])
                ins.then_inc(gn_step.sem, 1)
                dve.wait_ge(gn_mm.sem, 2 * n + 1)
                step_done(V.tensor_copy(gn_mean[:, b0:b1], scores[:, b0:b1]))
                step_done(V.tensor_tensor(gn_dev[:, b0:b1], gn_mv[:, b0:b1, 0], gn_mean[:, b0:b1], ALU.subtract))
                step_done(V.tensor_tensor(gn_dev[:, b0:b1], gn_dev[:, b0:b1], gn_dev[:, b0:b1], ALU.mult))
                V.tensor_tensor(gn_dev[:, b0:b1], gn_dev[:, b0:b1], gn_mv[:, b0:b1, 1], ALU.add
                                ).then_inc(gn_step.sem, 1)
                dve.wait_ge(gn_mm.sem, 2 * n + 2)
                V.tensor_scalar(gn_ve[:, b0:b1], scores[:, b0:b1], EPS, None, ALU.add).then_inc(gn_step.sem, 1)
                dve.wait_ge(gn_pow.sem, n + 1)
                step_done(V.tensor_scalar(gn_scale[:, b0:b1], gn_rstd[:, b0:b1], col[:, GNW:GNW + 1], None, ALU.mult))
                step_done(V.tensor_tensor(gn_bias[:, b0:b1], gn_mean[:, b0:b1], gn_scale[:, b0:b1], ALU.mult))
                V.tensor_scalar(gn_bias[:, b0:b1], gn_bias[:, b0:b1], -1.0, col[:, GNB:GNB + 1], ALU.mult, ALU.add
                                ).then_inc(gn_ready.sem, 1)

            dve.wait_ge(attn_w_in.sem, 16 * 7)
            group_norm(0, 0, 1)
            group_norm(1, 1, BATCH)

            dve.wait_ge(prep_mm.sem, 1)
            step_done(V.tensor_scalar(wpT[:, :], turn[0][:, 0:P], 1.0, None, ALU.mult))
            step_done(V.tensor_scalar(key_query_hi[:, :], turn[0][:, P:2 * P], SCORE_SCALE, None, ALU.mult))
            V.scalar_tensor_tensor(key_query_lo[:, :], turn[0][:, P:2 * P], SCORE_SCALE,
                                   key_query_hi[:, :].bitcast(F32), ALU.mult, ALU.subtract)
            V.tensor_scalar(col[:, QA:QA + 1], turn[0][:, 2 * P:2 * P + 1], SCORE_SCALE, None, ALU.mult
                            ).then_inc(prep_evac.sem, 1)
            dve.wait_ge(prep_mm.sem, 2)
            step_done(V.tensor_copy(value_proj_hi[:, :], turn[1][:, 0:P]))
            V.tensor_tensor(value_proj_lo[:, :], turn[1][:, 0:P], value_proj_hi[:, :].bitcast(F32), ALU.subtract)
            V.tensor_tensor(col[:, OB:OB + 1], turn[1][:, P:P + 1], col[:, PB:PB + 1], ALU.add
                            ).then_inc(prep_evac.sem, 1)

            def prepare(slot):
                if slot == 1:
                    dve.wait_ge(mamba_w_in.sem, 16 * 19)
                    V.tensor_scalar(alog[:, :], alog[:, :], A_LOG_MAX, None, ALU.min).then_inc(alog_clamped.sem, 1)
                    V.tensor_scalar(conv[:, :, :], conv[:, :, :], 0.5, None, ALU.mult)
                    V.tensor_scalar(half_se2b[:, :], col[:, SE2B:SE2B + 1], 0.5, None, ALU.mult)
                    dve.wait_ge(prep_mm.sem, 3)
                    V.tensor_copy(winT[:, :], mb[0][:, 0:INPROJ])
                    V.tensor_scalar(winTg[:, :], mb[0][:, 0:INPROJ], col[:, NG:NG + 1], None, ALU.mult
                                    ).then_inc(prep_evac.sem, 1)
                    dve.wait_ge(prep_mm.sem, 4)
                    V.tensor_scalar(woutT[:, :], mb[1][:, 0:P], col[:, RMSW:RMSW + 1], None, ALU.mult)
                    V.tensor_copy(se1T[:, :], mb[1][:, P:P + SE])
                    V.tensor_copy(se2T[:, :], mb[1][0:SE, 2 * P:3 * P]).then_inc(prep_evac.sem, 1)
                if slot == 3:
                    dve.wait_ge(a_exp_ready.sem, 1)
                    V.tensor_scalar(a_neg[:, :], a_exp[:, :], -A_SCALE, None, ALU.mult)
                    dve.wait_ge(prep_mm.sem, 5)
                    V.tensor_copy(winC[:, :], mb[2][:, 0:INPROJ])
                    V.tensor_tensor(dtb[:, :], mb[2][:, 400:400 + HEADS], dtb_in[:, :], ALU.add)
                    V.tensor_scalar(half_bz[:, :], mb[2][:, 408:409], 0.5, None, ALU.mult)
                    V.tensor_copy(col[:, BX:BBC + 1], mb[2][:, 410:412]).then_inc(prep_evac.sem, 1)

            def attn_setup(t):
                wait(dve, h_ready, t)
                wait(dve, scores_filled, t - 1, len(SCORE_USES))
                V.tensor_copy(h_hi[:, :], h32[:, :]).then_inc(h_split.sem, 1)
                wait(dve, h_split, t, 1)
                V.tensor_tensor(h_lo[:, :], h32[:, :], h_hi[:, :].bitcast(F32), ALU.subtract
                                ).then_inc(h_split.sem, 1)
                for n in range(2):
                    half = slice(n * HALF, (n + 1) * HALF)
                    wait(dve, q_hi_ready, t, n + 1)
                    V.scalar_tensor_tensor(q_lo[:, half], scores[:, half], col[:, QA:QA + 1],
                                           q_hi[:, half].bitcast(F32), ALU.add, ALU.subtract
                                           ).then_inc(q_lo_ready.sem, 1)
                for n in range(2):
                    wait(dve, v_hi_ready, t, n + 1)
                    V.tensor_tensor(v_lo[:, 4 * n:4 * n + 4, :], turn[n][:, :].rearrange("p (a b) -> p a b", a=4),
                                    v_hi[:, 4 * n:4 * n + 4, :].bitcast(F32), ALU.subtract
                                    ).then_inc(v_lo_ready.sem, 1)

            def attn_max(t, i):
                wait(dve, scores_filled, t, i + 2)
                V.tensor_reduce(neg_max[:, i:i + 1], scores[:, :], AX.X, ALU.max, negate=True
                                ).then_inc(max_ready.sem, 1)

            def attn_turned(t, i):
                g, i2 = divmod(i, 2)
                for n in range(2):
                    name = f"T{i}{'ab'[n]}"
                    wait(dve, pT_hi_ready, t, 2 * i + n + 1)
                    cols = slice(i2 * P, (i2 + 1) * P)
                    V.tensor_tensor(pT_lo[:, g % 2, 4 * n:4 * n + 4, cols],
                                    turn[turn_at[name][0]][:, :].rearrange("p (a b) -> p a b", a=4),
                                    pT_hi[:, g % 2, 4 * n:4 * n + 4, cols].bitcast(F32), ALU.subtract
                                    ).then_inc(pT_lo_ready.sem, 1)

            def attn_inv_rows(t, h):
                cols = slice(4 * h, 4 * h + 4)
                wait(dve, exp_done, t, 4 * h + 4)
                attn_dve.link(dve, V.reciprocal(inv[:, cols], row_sum[:, cols]))
                attn_dve.link(dve, V.tensor_copy(inv_rows[:, 0, cols].bitcast(F32R), inv[:, cols]))
                V.tensor_tensor(inv_rows[:, 1, cols], inv[:, cols], inv_rows[:, 0, cols], ALU.subtract
                                ).then_inc(inv_rows_ready.sem, 1)

            def attn_inv_T(t, h):
                bank = turn_take(dve, t, "invT" if h == 0 else "invT1")
                V.tensor_copy(inv_T[:, :], bank[0:64, 0:P]).then_inc(inv_T_ready.sem, 1)

            def attn_norm(t, h):
                half = slice(h * HALF, (h + 1) * HALF)
                wait(dve, x1res_ready, t - 1)
                wait(dve, pv_done, t, 2 * h + 2)
                wait(dve, inv_b_ready, t, h + 1)
                V.tensor_tensor(x1[:, half], attn_out[:, :], inv_b[:, :], ALU.mult).then_inc(out_taken.sem, 1)
                wait(dve, out_taken, t, h + 1)
                V.scalar_tensor_tensor(x1[:, half], x1[:, half], col[:, OB:OB + 1],
                                       x_all[:, bass.ds(t * TOKENS + h * HALF, HALF)], ALU.add, ALU.add
                                       ).then_inc(x1_ready.sem, 1)

            def attention(t, slot):
                if slot == 0:
                    attn_dve.start(t)
                    attn_setup(t)
                if slot == 7:
                    attn_norm(t, 0)
                if slot < TILES:
                    attn_max(t, slot)
                if slot == 5:
                    attn_inv_rows(t, 0)
                if slot == 8:
                    attn_inv_rows(t, 1)
                if 1 <= slot <= 8:
                    attn_turned(t, slot - 1)
                if slot == 5:
                    attn_inv_T(t, 0)
                if slot == 8:
                    attn_inv_T(t, 1)
                if slot == 9:
                    attn_norm(t, 1)
                    attn_dve.end()

            def rows_split(rows, value, last):
                n = value.shape[1]
                mamba_dve.link(dve, V.tensor_copy(rows[:, 0, 0:n].bitcast(F32R), value))
                V.tensor_tensor(rows[:, 1, 0:n], value, rows[:, 0, 0:n], ALU.subtract).then_inc(last.sem, 1)

            def convolve(t, k):
                w = conv[:, k, :]
                mamba_dve.link(dve, V.tensor_scalar(pre[:, k, :], raw[:, k, 0:TOKENS], w[:, 0:1],
                                                    w[:, TAPS:TAPS + 1], ALU.mult, ALU.add))
                for j in range(1, TAPS):
                    ins = V.scalar_tensor_tensor(pre[:, k, :], raw[:, k, j:j + TOKENS], w[:, j:j + 1],
                                                 pre[:, k, :], ALU.mult, ALU.add)
                    if j < TAPS - 1:
                        mamba_dve.link(dve, ins)
                    else:
                        ins.then_inc(pre_ready.sem, 1)

            def mamba(t, step):
                link = lambda ins: mamba_dve.link(dve, ins)
                if step == "x1T":
                    mamba_dve.start(t)
                    for n in range(2):
                        bank = mamba_take(dve, t, f"xT{n}")
                        for c in range(4):
                            ins = V.bn_stats(ln_raw[:, 4 * n + c, :], bank[:, c * P:(c + 1) * P])
                        ins.then_inc(ln_stats.sem, 1)
                    wait(dve, ln_stats, t, 2, dve_passed)
                    for c in range(TILES):
                        ins = V.bn_aggr(ln_mv[:, c, :], ln_raw[:, c, :])
                    link(ins)
                    V.tensor_scalar(ln_ve[:, :], ln_mv[:, :, 1], EPS, None, ALU.add).then_inc(ln_ve_ready.sem, 1)
                elif step == "ln_rows":
                    wait(dve, ln_rstd_ready, t)
                    rows_split(ln_rows, ln_rstd[:, :], ln_rows_ready)
                    bank = mamba_take(dve, t, "rT")
                    V.tensor_copy(ln_T[:, :], bank[0:64, 0:P]).then_inc(ln_T_ready.sem, 1)
                elif step == "ln_bcast":
                    for n in range(2):
                        half = slice(n * HALF, (n + 1) * HALF)
                        bank = mamba_take(dve, t, f"rB{n}")
                        V.tensor_tensor(u[:, half], bank[:, :], x1[:, half], ALU.mult).then_inc(u_ready.sem, 1)
                elif step == "dt_in":
                    bank = mamba_take(dve, t, "dt")
                    V.tensor_tensor(dtx[:, :].rearrange("p (c h) -> p c h", h=HEADS),
                                    bank[:, 0:N32].rearrange("p (c h) -> p c h", h=HEADS),
                                    dtb[:, :].unsqueeze(1).broadcast_to([P, TILES, HEADS]), ALU.add
                                    ).then_inc(dtx_ready.sem, 1)
                    wait(dve, dtx_ready, t)
                    V.scalar_tensor_tensor(dta[:, :], dtx[:, :], -1.0, dtx[:, :], ALU.mult, ALU.max
                                           ).then_inc(dta_ready.sem, 1)
                elif step == "conv_x":
                    wait(dve, raw_ready, t, 2)
                    convolve(t, 0)
                elif step == "dt":
                    wait(dve, dte_ready, t)
                    e, s, s2, acc = dtw[:, 0, :], dtw[:, 1, :], dtw[:, 2, :], dtw[:, 3, :]
                    link(V.tensor_scalar(e, dte[:, :], 2.0, None, ALU.add))
                    link(V.reciprocal(s, e))
                    link(V.tensor_tensor(s, s, dte[:, :], ALU.mult))
                    link(V.tensor_tensor(s2, s, s, ALU.mult))
                    link(V.tensor_scalar(acc, s2, 1.0 / 15, None, ALU.mult))
                    for odd in (13, 11, 9, 7, 5, 3):
                        link(V.scalar_tensor_tensor(acc, acc, 1.0 / odd, s2, ALU.add, ALU.mult))
                    link(V.scalar_tensor_tensor(acc, acc, 1.0, s, ALU.add, ALU.mult))
                    link(V.tensor_scalar(e, dtx[:, :], 0.0, None, ALU.max))
                    link(V.scalar_tensor_tensor(dt[:, :], acc, 2.0, e, ALU.mult, ALU.add))
                    link(V.tensor_tensor(dtw[:, 4, :].rearrange("p (c h) -> p c h", h=HEADS),
                                         dt[:, :].rearrange("p (c h) -> p c h", h=HEADS),
                                         a_neg[:, :].unsqueeze(1).broadcast_to([P, TILES, HEADS]), ALU.mult))
                    V.tensor_scalar(dtw[:, 4, :], dtw[:, 4, :], DA_LOG_MIN * A_SCALE, None, ALU.max
                                    ).then_inc(da_log_ready.sem, 1)
                elif step == "xs":
                    wait(dve, th_ready, t, 1)
                    V.scalar_tensor_tensor(xs[:, :], th[:, 0, :], 1.0, pre[:, 0, :], ALU.add, ALU.mult
                                           ).then_inc(xs_ready.sem, 1)
                elif step == "dA_rows":
                    wait(dve, dA_ready, t)
                    rows_split(dA_rows, dA[:, :], dA_rows_ready)
                    bank = mamba_take(dve, t, "dAT")
                    V.tensor_copy(dA_T[:, :], bank[0:64, 0:P]).then_inc(dA_T_ready.sem, 1)
                    V.tensor_tensor(dA_Tz[:, :], bank[0:64, 0:P], past_first[:, :], ALU.mult
                                    ).then_inc(dA_T_ready.sem, 1)
                elif step == "conv_bc":
                    wait(dve, raw_ready, t, 4)
                    convolve(t, 1)
                    wait(dve, th_ready, t, 2)
                    V.scalar_tensor_tensor(B[:, :], th[0:STATE, 1, :], 1.0, pre[0:STATE, 1, :], ALU.add, ALU.mult)
                    V.scalar_tensor_tensor(C[:, :], th[STATE:P, 1, :], 1.0, pre[STATE:P, 1, :], ALU.add, ALU.mult
                                           ).then_inc(bc_ready.sem, 1)
                elif step == "decay":
                    wait(dve, out_sent, t - 1, 16)
                    for c in range(TILES):
                        bank = mamba_take(dve, t, f"cd{c // 4}")
                        V.tensor_tensor_scan(decay_in[:, c * P:(c + 1) * P], bank[:, (c % 4) * P:(c % 4 + 1) * P],
                                             zeros[:, :], 1.0, ALU.mult, ALU.add).then_inc(decay_ready.sem, 1)
                elif step == "xsT":
                    for n in range(2):
                        bank = mamba_take(dve, t, f"xsT{n}")
                        part = slice(16 * n, 16 * n + 16)
                        V.tensor_tensor(xdt[:, part, :], bank[:, :].rearrange("p (a b) -> p a b", b=HEADDIM),
                                        dt[:, part].unsqueeze(2).broadcast_to([P, 16, HEADDIM]), ALU.mult
                                        ).then_inc(xdt_ready.sem, 1)
                elif step[0] == "L":
                    c = int(step[1])
                    bank = mamba_take(dve, t, f"Lb{c}")
                    V.tensor_tensor_scan(L[:, 4 * c:4 * c + 4, :].rearrange("p a b -> p (a b)"), bank[:, :],
                                         ident4[:, :, :].rearrange("p a b -> p (a b)"), 0.0, ALU.mult, ALU.add
                                         ).then_inc(L_ready.sem, 1)
                elif step[0] == "G":
                    n = int(step[1])
                    bank = mamba_take(dve, t, step)
                    wait(dve, L_ready, t, TILES)
                    wait(dve, xend_ready, t)
                    for c in range(4 * n, 4 * n + 4):
                        V.tensor_tensor(M[:, 4 * c:4 * c + 4, :], L[:, 4 * c:4 * c + 4, :],
                                        bank[:, (c % 4) * P:(c % 4 + 1) * P].unsqueeze(1).broadcast_to([P, HEADS, P]),
                                        ALU.mult).then_inc(M_ready.sem, 1)
                elif step == "U":
                    wait(dve, xdt_ready, t, 2)
                    wait(dve, L_ready, t, TILES)
                    V.tensor_tensor(xend[:, :, :], xdt[:, :, :], L[:, :, P - 1:P].broadcast_to([P, N32, HEADDIM]),
                                    ALU.mult).then_inc(xend_ready.sem, 1)
                    bank = mamba_take(dve, t, "U")
                    wait(dve, decay_ready, t, TILES)
                    V.tensor_copy(state[:, 1, :], bank[:, 0:STATE]).then_inc(state_ready.sem, 1)
                    for c in range(1, TILES - 1):
                        wait(dve, state_ready, t, c)
                        V.scalar_tensor_tensor(state[:, c + 1, :], state[:, c, :],
                                               decay_in[:, (c + 1) * P - 1:(c + 1) * P],
                                               bank[:, c * STATE:(c + 1) * STATE], ALU.mult, ALU.add
                                               ).then_inc(state_ready.sem, 1)
                elif step == "Y":
                    for n in range(2):
                        part = slice(P, HALF) if n == 0 else slice(HALF, TOKENS)
                        bank = mamba_take(dve, t, f"Yo{n}")
                        V.tensor_tensor(yo[:, part], bank[:, P if n == 0 else 0:HALF], decay_in[:, part], ALU.mult
                                        ).then_inc(yo_ready.sem, 1)
                    wait(dve, xs_ready, t)
                    for n in range(2):
                        half = slice(n * HALF, (n + 1) * HALF)
                        bank = mamba_take(dve, t, f"Y{n}")
                        V.scalar_tensor_tensor(y[:, half], xs[:, half], col[:, DP:DP + 1], bank[:, :],
                                               ALU.mult, ALU.add).then_inc(y_ready.sem, 1)
                    wait(dve, y_ready, t, 2)
                    wait(dve, yo_ready, t, 2)
                    link(V.tensor_tensor(y[:, P:TOKENS], y[:, P:TOKENS], yo[:, P:TOKENS], ALU.add))
                    wait(dve, gate_ready, t)
                    V.tensor_tensor(y2[:, :], y[:, :], gate[:, :], ALU.mult).then_inc(y2_ready.sem, 1)
                elif step == "y_rows":
                    bank = mamba_take(dve, t, "ss")
                    V.tensor_scalar(ms[:, :], bank[:, 0:TILES], 1.0 / P, EPS, ALU.mult, ALU.add
                                    ).then_inc(ms_ready.sem, 1)
                    wait(dve, y_rstd_ready, t)
                    rows_split(y_rows, y_rstd[:, :], y_rows_ready)
                    bank = mamba_take(dve, t, "yrT")
                    V.tensor_copy(y_T[:, :], bank[0:64, 0:P]).then_inc(y_T_ready.sem, 1)
                elif step == "out":
                    for n in range(2):
                        half = slice(n * HALF, (n + 1) * HALF)
                        wait(dve, y_b_ready, t, n + 1)
                        bank = mamba_take(dve, t, f"out{n}")
                        V.tensor_tensor_reduce(out=o_img[:, half], in0=bank[:, :], in1=y_b[:, half], scale=1.0,
                                               scalar=0.0, op0=ALU.mult, op1=ALU.add,
                                               accum_out=pooled[:, n:n + 1]).then_inc(pooled_ready.sem, 1)
                elif step == "fin":
                    wait(dve, tha_ready, t)
                    link(V.tensor_scalar(att[:, :], tha[:, :], 1.0, 0.5, ALU.add, ALU.mult))
                    wait(dve, x1res_ready, t)
                    wait(dve, pooled_ready, t, 2)
                    V.scalar_tensor_tensor(fin[:, :], o_img[:, :], att[:, :], x1res[:, :], ALU.mult, ALU.add
                                           ).then_inc(fin_ready.sem, 1)
                    mamba_dve.end()

            run_streams(dve, attention, mamba, prepare)

        @block.tensor
        def _(pe):
            T = nc.tensor

            def mm(o, w, v, start=True, stop=True):
                return T.matmul(o, w, v, start=start, stop=stop)

            def mm3(o, w_hi, w_lo, v_hi, v_lo, start=True, stop=True):
                mm(o, w_hi, v_hi, start, False)
                mm(o, w_hi, v_lo, False, False)
                return mm(o, w_lo, v_hi, False, stop)

            pe.wait_ge(consts_done.sem, 11)
            for n, (b0, b1) in enumerate(((0, 1), (1, BATCH))):
                pe.wait_ge(gn_step.sem, 3 * n + 1)
                mm(scores[:, b0:b1], group_avg[:, :], gn_mv[:, b0:b1, 0]).then_inc(gn_mm.sem, 1)
                pe.wait_ge(gn_step.sem, 3 * n + 2)
                mm(scores[:, b0:b1], group_avg[:, :], gn_dev[:, b0:b1]).then_inc(gn_mm.sem, 1)
            pe.wait_ge(attn_w_in.sem, 16 * 7)
            T.transpose(turn[0][:, 0:P], wp[:, :], ident[:, :])
            mm(turn[0][:, P:2 * P], wqkv[:, 0, :], wqkv[:, 1, :])
            mm(turn[0][:, 2 * P:2 * P + 1], wqkv[:, 1, :], col[:, QB:QB + 1]).then_inc(prep_mm.sem, 1)
            pe.wait_ge(prep_evac.sem, 1)
            mm(turn[1][:, 0:P], wqkv[:, 2, :], wpT[:, :])
            mm(turn[1][:, P:P + 1], wpT[:, :], col[:, VB:VB + 1]).then_inc(prep_mm.sem, 1)
            pe.wait_ge(prep_evac.sem, 2)

            def prepare(slot):
                if slot == 0:
                    pe.wait_ge(mamba_w_in.sem, 16 * 19)
                    for k in range(3):
                        T.transpose(mb[0][:, k * P:(k + 1) * P], win[:, k, :], ident[:, :])
                    T.transpose(mb[0][:, 3 * P:INPROJ], win[0:HEADS, 3, :], ident[0:HEADS, 0:HEADS]
                                ).then_inc(prep_mm.sem, 1)
                    T.transpose(mb[1][:, 0:P], wout[:, :], ident[:, :])
                    T.transpose(mb[1][:, P:P + SE], wse1[:, :], ident[0:SE, 0:SE])
                    T.transpose(mb[1][0:SE, 2 * P:3 * P], wse2[:, :], ident[:, :]).then_inc(prep_mm.sem, 1)
                if slot == 1:
                    pe.wait_ge(prep_evac.sem, 4)
                    mm(mb[2][:, 0:INPROJ], center[:, :], winTg[:, :])
                    mm(mb[2][:, 400:400 + HEADS], col[:, NB:NB + 1].broadcast_to([P, P]), winT[:, 3 * P:INPROJ])
                    for k, at in ((0, 408), (1, 410), (2, 411)):
                        last = mm(mb[2][:, at:at + 1], winT[:, k * P:(k + 1) * P], col[:, NB:NB + 1])
                    last.then_inc(prep_mm.sem, 1)

            def attn_setup(t):
                wait(pe, h_split, t, 2)
                wait(pe, exp_done, t - 1, TILES)
                for n in range(2):
                    half = slice(n * HALF, (n + 1) * HALF)
                    last = mm3(scores[:, half], key_query_hi[:, :], key_query_lo[:, :], h_hi[:, half], h_lo[:, half])
                last.then_inc(scores_filled.sem, 1)
                for n in range(2):
                    bank, filled = turn_fill(pe, t, f"V{n}")
                    for c in range(4):
                        tile = slice((4 * n + c) * P, (4 * n + c + 1) * P)
                        last = mm3(bank[:, c * P:(c + 1) * P], h_hi[:, tile], h_lo[:, tile],
                                   value_proj_hi[:, :], value_proj_lo[:, :])
                    last.then_inc(filled, 1)

            def attn_scores(t, i):
                if i == 0:
                    wait(pe, q_lo_ready, t, 2)
                else:
                    wait(pe, exp_done, t, i)
                tile = slice(i * P, (i + 1) * P)
                for n in range(2):
                    half = slice(n * HALF, (n + 1) * HALF)
                    last = mm3(scores[:, half], q_hi[:, tile], q_lo[:, tile], h_hi[:, half], h_lo[:, half])
                last.then_inc(scores_filled.sem, 1)

            def attn_turn(t, i):
                wait(pe, exp_done, t, i + 1)
                for n in range(2):
                    bank, filled = turn_fill(pe, t, f"T{i}{'ab'[n]}")
                    for c in range(4):
                        last = T.transpose(bank[:, c * P:(c + 1) * P],
                                           probs[:, i % 2, (4 * n + c) * P:(4 * n + c + 1) * P], ident[:, :])
                    last.then_inc(filled, 1)

            def attn_values(t, g, k0, k1):
                if k0 == 0:
                    wait(pe, pT_lo_ready, t, 4 * g + 4)
                    wait(pe, v_lo_ready, t, 2)
                    wait(pe, out_taken, t, g // 2)
                b = g % 2
                for k in range(k0, k1):
                    last = mm3(attn_out[:, b * 2 * P:(b + 1) * 2 * P], v_hi[:, k, :], v_lo[:, k, :],
                               pT_hi[:, b, k, :], pT_lo[:, b, k, :], k == 0, k == TILES - 1)
                if k1 == TILES:
                    last.then_inc(pv_done.sem, 1)

            def attn_inv_T(t, h):
                wait(pe, inv_rows_ready, t, h + 1)
                bank, filled = turn_fill(pe, t, "invT" if h == 0 else "invT1", pe_passed)
                T.transpose(bank[0:64, 0:P], inv_rows[:, :, :].rearrange("p a b -> p (a b)"), ident[:, :]
                            ).then_inc(filled, 1)

            def attn_inv_b(t, h):
                wait(pe, inv_T_ready, t, h + 1)
                bank, filled = turn_fill(pe, t, "invB" if h == 0 else "invB1")
                for c in range(4):
                    last = mm(bank[:, c * P:(c + 1) * P], pick(4 * h + c), inv_T[:, :])
                last.then_inc(filled, 1)

            def pick(r):
                return pick_row[:, r:r + 1].broadcast_to([64, P])

            def attention(t, slot):
                if slot == 0:
                    attn_setup(t)
                if slot < TILES:
                    attn_scores(t, slot)
                if slot == 6:
                    attn_inv_b(t, 0)
                if 1 <= slot <= 8:
                    attn_turn(t, slot - 1)
                if slot == 5:
                    attn_inv_T(t, 0)
                if 3 <= slot <= 8:
                    g, part = divmod(slot - 3, 2)
                    attn_values(t, g, 4 * part, 4 * part + 4)
                if slot == 8:
                    attn_inv_T(t, 1)
                    attn_inv_b(t, 1)
                if slot == 9:
                    attn_values(t, 3, 0, TILES)

            def mamba(t, step):
                if step == "x1T":
                    for n in range(2):
                        wait(pe, x1_ready, t, n + 1)
                        bank, filled = mamba_fill(pe, t, f"xT{n}")
                        for c in range(4):
                            tile = slice((4 * n + c) * P, (4 * n + c + 1) * P)
                            last = T.transpose(bank[:, c * P:(c + 1) * P], x1[:, tile], ident[:, :])
                        last.then_inc(filled, 1)
                elif step == "ln_rows":
                    wait(pe, ln_rows_ready, t)
                    bank, filled = mamba_fill(pe, t, "rT", pe_passed)
                    T.transpose(bank[0:64, 0:P], ln_rows[:, :, :].rearrange("p a b -> p (a b)"), ident[:, :]
                                ).then_inc(filled, 1)
                elif step == "ln_bcast":
                    wait(pe, ln_T_ready, t)
                    for n in range(2):
                        bank, filled = mamba_fill(pe, t, f"rB{n}")
                        for c in range(4):
                            last = mm(bank[:, c * P:(c + 1) * P], pick(4 * n + c), ln_T[:, :])
                        last.then_inc(filled, 1)
                elif step in ("in_x", "in_bc", "in_z"):
                    name, k = {"in_x": ("inx", 1), "in_bc": ("inbc", 2), "in_z": ("inz", 0)}[step]
                    for n in range(2):
                        wait(pe, u_ready, t, n + 1)
                        bank, filled = mamba_fill(pe, t, f"{name}{n}")
                        mm(bank[:, :], winC[:, k * P:(k + 1) * P], u[:, n * HALF:(n + 1) * HALF]).then_inc(filled, 1)
                elif step == "dt_in":
                    bank, filled = mamba_fill(pe, t, "dt")
                    for c in range(TILES):
                        last = mm(bank[:, c * HEADS:(c + 1) * HEADS], u[:, c * P:(c + 1) * P], winC[:, 3 * P:INPROJ])
                    last.then_inc(filled, 1)
                elif step == "dA_rows":
                    wait(pe, dA_rows_ready, t)
                    bank, filled = mamba_fill(pe, t, "dAT", pe_passed)
                    T.transpose(bank[0:64, 0:P], dA_rows[:, :, :].rearrange("p a b -> p (a b)"), ident[:, :]
                                ).then_inc(filled, 1)
                elif step == "decay":
                    wait(pe, dA_T_ready, t, 2)
                    for n in range(2):
                        bank, filled = mamba_fill(pe, t, f"cd{n}")
                        for c in range(4):
                            last = mm(bank[:, c * P:(c + 1) * P], pick_head[:, 4 * n + c, :], dA_T[:, :])
                        last.then_inc(filled, 1)
                elif step == "xsT":
                    wait(pe, xs_ready, t)
                    for n in range(2):
                        bank, filled = mamba_fill(pe, t, f"xsT{n}")
                        for c in range(4):
                            tile = slice((4 * n + c) * P, (4 * n + c + 1) * P)
                            last = T.transpose(bank[:, c * P:(c + 1) * P], xs[:, tile], ident[:, :])
                        last.then_inc(filled, 1)
                elif step == "BT":
                    wait(pe, bc_ready, t)
                    bank, filled = mamba_fill(pe, t, "BT", pe_passed)
                    for c in range(TILES):
                        last = T.transpose(bank[:, c * STATE:(c + 1) * STATE], B[:, c * P:(c + 1) * P],
                                           ident[0:STATE, 0:STATE])
                    last.then_inc(filled, 1)
                elif step[0] == "L":
                    c = int(step[1])
                    bank, filled = mamba_fill(pe, t, f"Lb{c}")
                    for h in range(HEADS):
                        last = mm(bank[:, h * P:(h + 1) * P], pick(HEADS * c + h), dA_Tz[:, :])
                    last.then_inc(filled, 1)
                elif step[0] == "G":
                    bank, filled = mamba_fill(pe, t, step)
                    for c in range(4):
                        tile = slice((4 * int(step[1]) + c) * P, (4 * int(step[1]) + c + 1) * P)
                        last = mm(bank[:, c * P:(c + 1) * P], B[:, tile], C[:, tile])
                    last.then_inc(filled, 1)
                elif step == "U":
                    wait(pe, xend_ready, t)
                    wait(pe, BT_ready, t)
                    bank, filled = mamba_fill(pe, t, "U")
                    for c in range(TILES):
                        last = mm(bank[:, c * STATE:(c + 1) * STATE],
                                  xend[:, 4 * c:4 * c + 4, :].rearrange("p a b -> p (a b)"), BT[:, c, :])
                    last.then_inc(filled, 1)
                elif step == "stateT":
                    for n in range(2):
                        wait(pe, state_ready, t, 3 if n == 0 else TILES - 1)
                        bank, filled = mamba_fill(pe, t, f"ST{n}", pe_passed)
                        for c in range(1 if n == 0 else 0, 4):
                            last = T.transpose(bank[0:STATE, c * P:(c + 1) * P], state[:, 4 * n + c, :], ident[:, :])
                        last.then_inc(filled, 1)
                elif step == "Y":
                    for n in range(2):
                        wait(pe, stateT_ready, t, n + 1)
                        bank, filled = mamba_fill(pe, t, f"Yo{n}")
                        for c in range(1 if n == 0 else 0, 4):
                            tile = slice((4 * n + c) * P, (4 * n + c + 1) * P)
                            last = mm(bank[:, c * P:(c + 1) * P], stateT[:, 4 * n + c, :], C[:, tile])
                        last.then_inc(filled, 1)
                    for n in range(2):
                        wait(pe, M_ready, t, 4 * n + 4)
                        bank, filled = mamba_fill(pe, t, f"Y{n}")
                        for c in range(4):
                            for h in range(HEADS):
                                r = HEADS * (4 * n + c) + h
                                last = mm(bank[h * HEADDIM:(h + 1) * HEADDIM, c * P:(c + 1) * P], xdt[:, r, :],
                                          M[:, r, :])
                        last.then_inc(filled, 1)
                elif step == "y_rows":
                    wait(pe, sq_ready, t)
                    bank, filled = mamba_fill(pe, t, "ss")
                    for c in range(TILES):
                        last = mm(bank[:, c:c + 1], sq[:, c * P:(c + 1) * P], ones[:, :])
                    last.then_inc(filled, 1)
                    wait(pe, y_rows_ready, t)
                    bank, filled = mamba_fill(pe, t, "yrT", pe_passed)
                    T.transpose(bank[0:64, 0:P], y_rows[:, :, :].rearrange("p a b -> p (a b)"), ident[:, :]
                                ).then_inc(filled, 1)
                elif step == "out":
                    wait(pe, y_T_ready, t)
                    for n in range(2):
                        bank, filled = mamba_fill(pe, t, f"yrB{n}")
                        for c in range(4):
                            last = mm(bank[:, c * P:(c + 1) * P], pick(4 * n + c), y_T[:, :])
                        last.then_inc(filled, 1)
                    for n in range(2):
                        bank, filled = mamba_fill(pe, t, f"out{n}")
                        mm(bank[:, :], woutT[:, :], y2[:, n * HALF:(n + 1) * HALF]).then_inc(filled, 1)
                elif step == "se":
                    wait(pe, pooled_ready, t, 2)
                    bank, filled = mamba_fill(pe, t, "se1")
                    mm(bank[0:SE, 0:1], se1T[:, :], pooled[:, 0:1], True, False)
                    mm(bank[0:SE, 0:1], se1T[:, :], pooled[:, 1:2], False, True).then_inc(filled, 1)
                    wait(pe, hdn_ready, t)
                    bank, filled = mamba_fill(pe, t, "se2")
                    mm(bank[:, 0:1], se2T[:, :], hdn[:, :]).then_inc(filled, 1)

            run_streams(pe, attention, mamba, prepare)


INPUTS = ["x", "L0_conv_gn_w", "L0_conv_gn_b", "L0_conv_qkv_w", "L0_conv_qkv_b", "L0_conv_proj_w",
          "L0_conv_proj_b", "L1_conv_norm_g", "L1_conv_norm_b", "L1_conv_in_w", "L1_conv_conv_w",
          "L1_conv_conv_b", "L1_conv_dt_bias", "L1_conv_A_log", "L1_conv_Dp", "L1_conv_rms_w",
          "L1_conv_out_w", "L1_conv_se1_w", "L1_conv_se1_b", "L1_conv_se2_w", "L1_conv_se2_b"]


def kernel(**inputs):
    import numpy as np
    import concourse.bacc as bacc
    from concourse.bass_utils import run_bass_kernel_spmd

    nc = bacc.Bacc("TRN2", target_bir_lowering=False, num_devices=1)
    arrays, args = {}, []
    for name in INPUTS:
        a = np.ascontiguousarray(inputs[name])
        arrays[f"in_{name}"] = a
        args.append(nc.dram_tensor(f"in_{name}", a.shape, mybir.dt.from_np(a.dtype), kind="ExternalInput").ap())
    shape = arrays["in_x"].shape
    out = nc.dram_tensor("out", shape, F32, kind="ExternalOutput").ap()
    build(nc, *args, out)
    r = run_bass_kernel_spmd(nc, [arrays], core_ids=[0])
    return r.results[0]["out"]
```

```python
from contextlib import ExitStack

import concourse.bass as bass
from concourse import mybir

F32 = mybir.dt.float32
F32R = mybir.dt.float32r
ALU = mybir.AluOpType
ACT = mybir.ActivationFunctionType
AX = mybir.AxisListType

P = 128
BATCH = 4
TOKENS = 1024
TILES = TOKENS // P
HALF = 512
GROUPS = 8
HEADS = 4
HEADDIM = 32
STATE = 64
TAPS = 4
SE = 32
INPROJ = 2 * P + 2 * STATE + HEADS
EPS = 1e-5
SCORE_SCALE = float(P) ** -0.5
A_LOG_MAX = 88.0
A_SCALE = 2.0 ** -40
DA_LOG_MIN = -200.0


class Signal:

    def __init__(self, sem, per_batch):
        self.sem, self.per_batch = sem, per_batch

    def at(self, t, k):
        return t * self.per_batch + k


def wait(eng, signal, t, k=1, beside=None):
    value = signal.at(t, k)
    if isinstance(value, int):
        if value <= 0:
            return
    eng.wait_ge(signal.sem, value)
    if beside is not None:
        eng.sem_inc(beside, 1)


class Chain:

    def __init__(self, sem, per_batch):
        self.counter, self.k = Signal(sem, per_batch), 0

    def start(self):
        self.k = 0

    def before(self, eng, t):
        wait(eng, self.counter, t, self.k)

    def done(self, instruction):
        self.k += 1
        instruction.then_inc(self.counter.sem, 1)

    def end(self):
        assert self.k == self.counter.per_batch, (self.k, self.counter.per_batch)


FIRST_ORDER = """
h h_hi h_lo Q q_hi0 q_hi1 q_lo0 q_lo1 S0 S1 V0 S2 V1 max0 S3 exp0 v0 exp1 sum0 inv0 T0 exp2 exp3 pT0 v1
max1 S4 sum1 S5 inv1 scale0 scale1 scale2 scale3 T1 max2 pT1 exp4 S6 S7 T2 exp5 pT2 sum2 inv2 T3 max3
pT3 exp6 pT4 exp7 T4 S8 T5 PV0 sum3 inv3 T6 S9 T7 max4 PV1 pT5 pT6 exp8 pT7 exp9 exp10 exp11 S10 sum4
S11 inv4 scale4 scale5 scale6 scale7 max5 PV2 T8 sum5 inv5 max6 norm0 S12 pT8 S13 T9 T10 T11 PV3 pT9
pT10 exp12 exp13 sum6 S14 PV4 S15 inv6 max7 T12 T13 pT11 PV5 X1T0 pT12 pT13 exp14 exp15 sum7 inv7 T14
T15 pT14 PV6 PV7 norm1 keep0 pT15 keep1 X1T1 stats0 stats1 ln_ve ln_pow ln_rows LnT ln_T LnB0 LnB1 u0 u1
""".split()
ORDER = """
h InX0 InBC0 raw_x0 InX1 h_hi raw_bc0 InBC1 h_lo raw_x1 Dt conv_x0 conv_x1 Q dt_x conv_x2 V0 q_hi0 q_hi1
q_lo0 sp_exp raw_bc1 q_lo1 conv_bc0 sp0 sp1 S0 sp2 conv_x3 v0 S1 InZ0 sp3 max0 InZ1 sp4 exp0 sp5
conv_bc1 exp1 S2 z0 sp6 sum0 S3 sp7 inv0 conv_bc2 scale0 th_x max1 T0 V1 pT0 sp8 conv_bc3 exp2 exp3 S4
sp9 xs v1 S5 z1 T1 sp10 sum1 inv1 sp11 XsT0 scale1 sp12 max2 pT1 XsT1 th_bc sp13 T2 sp14 exp4 sp15 T3
silu_c exp5 S6 dA pT2 sum2 xdt0 S7 pT3 dA_rows PV0 inv2 xdt1 scale2 silu_b DAT T4 dA_T T5 max3 pT4
Decay0 Decay1 BT decay0 exp6 exp7 S8 pT5 sum3 decay1 S9 bt L0 inv3 max4 L1 scale3 L2 PV1 l0 exp8 gate0
l1 exp9 l2 L3 sum4 L4 l3 L5 S10 l4 L6 l5 T6 inv4 l6 L7 scale4 pT6 G0 l7 PV2 to_end m0 xend m1 m2 S11 m3
gate1 T7 max5 G1 U exp10 dx pT7 exp11 PV3 st0 st1 st2 st3 st4 m4 T8 S12 sum5 pT8 inv5 m5 scale5 T9 m6
S13 pT9 st5 norm0 T10 StT0 max6 pT10 T11 st_T0 PV4 pT11 st6 m7 exp12 Yo0 StT1 yo0 Y0 st_T1 yo_dx0 exp13
S14 sum6 inv6 y0 Yo1 scale6 g0 S15 yo1 sq0 T12 max7 Y1 yo_dx1 pT12 exp14 T13 y1 X1T0 exp15 PV5 g1 pT13
sum7 inv7 sq1 scale7 Ss T14 ms stats0 T15 y_pow pT14 pT15 PV6 keep0 y_rows PV7 YrT norm1 y_T X1T1 YrB0
stats1 Out0 y_b0 ln_ve YrB1 Out1 y_b1 o0 ln_pow keep1 o1 ln_rows LnT SeA ln_T hdn LnB0 LnB1 u0 SeB tha
att u1 fin0 fin1
""".split()
LAST_ORDER = """
InX0 InX1 raw_x0 InBC0 raw_x1 InZ0 conv_x0 Dt raw_bc0 conv_x1 InBC1 dt_x sp_exp z0 sp0 sp1 sp2 sp3
raw_bc1 sp4 InZ1 sp5 conv_x2 conv_bc0 sp6 sp7 z1 sp8 conv_x3 conv_bc1 th_x conv_bc2 sp9 sp10 xs sp11
conv_bc3 dx XsT0 sp12 th_bc sp13 gate0 sp14 sp15 xdt0 dA dA_rows silu_c DAT XsT1 dA_T xdt1 Decay0 Decay1
decay0 L0 decay1 L1 l0 L2 l1 L3 silu_b L4 l2 l3 BT l4 L5 bt L6 l5 L7 l6 G0 l7 to_end xend G1 m0 m1 gate1
m2 U m3 m4 m5 st0 st1 st2 m6 StT0 st3 st_T0 m7 st4 Yo0 st5 st6 StT1 yo0 Y0 st_T1 yo_dx0 Yo1 Y1 yo1 y0
yo_dx1 g0 sq0 y1 g1 sq1 Ss ms y_pow y_rows YrT Out0 y_T YrB0 YrB1 y_b0 o0 y_b1 Out1 o1 SeA hdn SeB tha
att fin0 fin1
""".split()
PREPARE = ["max0", "max1", "max2", "max3", "max4", "max5"]

ATTENTION = {"h", "h_hi", "h_lo", "Q", "q_hi", "q_lo", "V", "v", "S", "max", "exp", "sum", "inv", "scale",
             "T", "pT", "PV", "norm"}
MODEL_START = {"X1T", "stats", "ln_ve", "ln_pow", "ln_rows", "LnT", "ln_T", "LnB", "u", "keep"}


def parse(step):
    kind = step.rstrip("0123456789")
    return kind, int(step[len(kind):] or 0)


def batches_behind(kind):
    return 0 if kind in ATTENTION or kind in MODEL_START else 1


def phase(iteration):
    return {0: 0, BATCH: 2}.get(iteration, 1) if isinstance(iteration, int) else 1


ORDERS = [FIRST_ORDER, ORDER, LAST_ORDER]
SCORE_USES = [s for s in ORDER if parse(s)[0] in ("Q", "S")]
TURN_KINDS = ("V", "T")
TURN_USES = [[s for s in order if parse(s)[0] in TURN_KINDS] for order in ORDERS]
MAMBA_USES = [[s for s in order if s[0].isupper() and parse(s)[0] not in ATTENTION] for order in ORDERS]


def previous_use(uses, banks, name, iteration):
    now = uses[phase(iteration)]
    n = now.index(name)
    if n >= banks:
        return now[n - banks], 0
    if isinstance(iteration, int) and iteration == 0:
        return None, 0
    before = uses[phase(iteration - 1)]
    same_bank = before[n::banks]
    return (same_bank[-1], 1) if same_bank else (None, 0)


def build(nc, x, gn_w, gn_b, qkv_w, qkv_b, proj_w, proj_b, norm_g, norm_b, in_w, conv_w, conv_b, dt_bias,
          A_log, Dp, rms_w, out_w, se1_w, se1_b, se2_w, se2_b, out):
    x_d = x.rearrange("b c h w -> b c (h w)")
    out_d = out.rearrange("b c h w -> b c (h w)")

    with ExitStack() as ctx:
        def sb(name, shape, dt=F32):
            return ctx.enter_context(nc.sbuf_tensor(name, shape, dt))

        def signal(name, per_batch=1):
            return Signal(ctx.enter_context(nc.semaphore(name)), per_batch)

        scores = ctx.enter_context(nc.psum_tensor("scores", [P, TOKENS], F32))
        turn = [ctx.enter_context(nc.psum_tensor(f"turn{b}", [P, HALF], F32)) for b in range(2)]
        attn_out = ctx.enter_context(nc.psum_tensor("attn_out", [P, HALF], F32))
        mb = [ctx.enter_context(nc.psum_tensor(f"mamba{b}", [P, HALF], F32)) for b in range(3)]

        ident = sb("ident", [P, P])
        ident4 = sb("ident4", [P, HEADS, P])
        center = sb("center", [P, P])
        group_avg = sb("group_avg", [P, P])
        zeros = sb("zeros", [P, P])
        ones = sb("ones", [P, 1])
        past_first = sb("past_first", [2 * 32, P])
        neg_half = sb("neg_half", [P, TILES])
        pick_row = sb("pick_row", [2 * 32, 32], F32R)
        pick_head = sb("pick_head", [2 * 32, TILES, P], F32R)

        x_all = sb("x_all", [P, BATCH * TOKENS])
        wqkv = sb("wqkv", [P, 3, P])
        wp = sb("wp", [P, P])
        win = sb("win", [P, 4, P])
        wout = sb("wout", [P, P])
        wse1 = sb("wse1", [SE, P])
        wse2 = sb("wse2", [P, SE])
        (GNW, GNB, QB, VB, PB, NG, NB, RMSW, DP, SE2B, QA, OB, BZ, BX, BBC) = range(15)
        col = sb("col", [P, 15])
        se1b = sb("se1b", [SE, 1])
        conv = sb("conv", [P, 2, TAPS + 1])
        dtb_in = sb("dtb_in", [P, HEADS])
        alog = sb("alog", [P, HEADS])

        key_query_hi = sb("key_query_hi", [P, P], F32R)
        key_query_lo = sb("key_query_lo", [P, P], F32R)
        wpT = sb("wpT", [P, P])
        value_proj_hi = sb("value_proj_hi", [P, P], F32R)
        value_proj_lo = sb("value_proj_lo", [P, P], F32R)
        winT = sb("winT", [P, INPROJ])
        winTg = sb("winTg", [P, INPROJ])
        winC = sb("winC", [P, INPROJ])
        woutT = sb("woutT", [P, P])
        se1T = sb("se1T", [P, SE])
        se2T = sb("se2T", [SE, P])
        dtb = sb("dtb", [P, HEADS])
        a_exp = sb("a_exp", [P, HEADS])
        a_neg = sb("a_neg", [P, HEADS])
        half_bz = sb("half_bz", [P, 1])
        half_se2b = sb("half_se2b", [P, 1])

        gn_raw = sb("gn_raw", [P, BATCH, 2, 6])
        gn_mv = sb("gn_mv", [P, BATCH, 2])
        gn_mean = sb("gn_mean", [P, BATCH])
        gn_dev = sb("gn_dev", [P, BATCH])
        gn_ve = sb("gn_ve", [P, BATCH])
        gn_rstd = sb("gn_rstd", [P, BATCH])
        gn_scale = sb("gn_scale", [P, BATCH])
        gn_bias = sb("gn_bias", [P, BATCH])

        h32 = sb("h32", [P, TOKENS])
        h_hi = sb("h_hi", [P, TOKENS], F32R)
        h_lo = sb("h_lo", [P, TOKENS], F32R)
        q_hi = sb("q_hi", [P, TOKENS], F32R)
        q_lo = sb("q_lo", [P, TOKENS], F32R)
        values = sb("values", [P, TILES, P])
        neg_max = sb("neg_max", [P, TILES])
        row_sum = sb("row_sum", [P, 2, TILES])
        probs = sb("probs", [P, 2, TOKENS])
        pT = sb("pT", [P, 2, TILES, 2 * P])
        row_total = sb("row_total", [P, TILES])
        inv = sb("inv", [P, TILES])
        x1 = sb("x1", [P, TOKENS])

        ln_raw = sb("ln_raw", [P, TILES, 6])
        ln_mv = sb("ln_mv", [P, TILES, 2])
        ln_ve = sb("ln_ve", [P, TILES])
        ln_rstd = sb("ln_rstd", [P, TILES])
        ln_rows = sb("ln_rows", [P, 2, 32])
        ln_T = sb("ln_T", [2 * 32, P], F32R)
        u = sb("u", [P, TOKENS])
        PAD = TAPS - 1
        raw = sb("raw", [P, 2, PAD + TOKENS])
        pre = sb("pre", [P, 2, TOKENS])
        th = sb("th", [P, 2, TOKENS])
        xs = sb("xs", [P, TOKENS])
        B = sb("B", [STATE, TOKENS])
        C = sb("C", [STATE, TOKENS])
        thz = sb("thz", [P, TOKENS])
        zv = sb("zv", [P, TOKENS])
        gate = sb("gate", [P, TOKENS])
        N32 = TILES * HEADS
        dtx = sb("dtx", [P, N32])
        dta = sb("dta", [P, N32])
        dte = sb("dte", [P, N32])
        dtw = sb("dtw", [P, 6, N32])
        dt = sb("dt", [P, N32])
        dA = sb("dA", [P, N32])
        dA_rows = sb("dA_rows", [P, 2, 32])
        dA_T = sb("dA_T", [2 * 32, P], F32R)
        dA_Tz = sb("dA_Tz", [2 * 32, P], F32R)
        decay_in = sb("decay_in", [P, TOKENS])
        xdt = sb("xdt", [P, N32, HEADDIM])
        to_end = sb("to_end", [P, N32])
        xend = sb("xend", [P, N32, HEADDIM])
        BT = sb("BT", [P, TILES, STATE])
        L = sb("L", [P, N32, P])
        M = L
        state = sb("state", [P, TILES, STATE])
        stateT = sb("stateT", [STATE, TILES, P])
        yo = sb("yo", [P, TOKENS])
        y = sb("y", [P, TOKENS])
        y2 = xs
        sq = sb("sq", [P, TOKENS])
        dx = sq
        y_b = sb("y_b", [P, TOKENS])
        ms = sb("ms", [P, TILES])
        y_rstd = sb("y_rstd", [P, TILES])
        y_rows = sb("y_rows", [P, 2, 32])
        y_T = sb("y_T", [2 * 32, P], F32R)
        o_img = y
        pooled = sb("pooled", [P, 2])
        hdn = sb("hdn", [SE, 1])
        tha = sb("tha", [P, 1])
        att = sb("att", [P, 1])
        fin = o_img

        x_in = [signal(f"x_in{b}") for b in range(BATCH)]
        attn_w_in = signal("attn_w_in")
        mamba_w_in = signal("mamba_w_in")
        consts_done = signal("consts_done")
        pool_step = signal("pool_step")
        gn_step = signal("gn_step")
        gn_mm = signal("gn_mm")
        gn_pow = signal("gn_pow")
        gn_ready = signal("gn_ready")
        prep_mm = signal("prep_mm")
        prep_evac = signal("prep_evac")
        dve_prep = signal("dve_prep")
        alog_clamped, a_exp_ready = signal("alog_clamped"), signal("a_exp_ready")
        scores_filled = signal("scores_filled", len(SCORE_USES))
        pe_passed, dve_passed, pool_passed, act_passed = (ctx.enter_context(nc.semaphore(n))
                                              for n in ("pe_passed", "dve_passed", "pool_passed", "act_passed"))
        filled = {kind: signal(f"{kind}_filled", sum(parse(s)[0] == kind for s in ORDER))
                  for kind in sorted({parse(s)[0] for s in TURN_USES[1] + MAMBA_USES[1]})}
        h_ready = signal("h_ready")
        h_split = signal("h_split", 2)
        q_hi_ready, q_lo_ready = signal("q_hi_ready", 2), signal("q_lo_ready", 2)
        v_ready = signal("v_ready", 2)
        max_ready = signal("max_ready", TILES)
        exp_done = signal("exp_done", 2 * TILES)
        pT_ready = signal("pT_ready", 2 * TILES)
        pv_done = signal("pv_done", 4)
        summed, inv_ready = signal("summed", TILES), signal("inv_ready", TILES)
        scaled = signal("scaled", TILES)
        x1_ready, x1_kept = signal("x1_ready", 2), signal("x1_kept", 2)
        ln_stats = signal("ln_stats", 2)
        ln_ve_ready, ln_rstd_ready = signal("ln_ve_ready"), signal("ln_rstd_ready")
        ln_rows_ready, ln_T_ready = signal("ln_rows_ready"), signal("ln_T_ready")
        u_ready = signal("u_ready", 2)
        raw_x_ready, raw_bc_ready = signal("raw_x_ready", 2), signal("raw_bc_ready", 2)
        tap_x, tap_bc = signal("tap_x", TAPS), signal("tap_bc", TAPS)
        th_x_ready, th_bc_ready = signal("th_x_ready"), signal("th_bc_ready")
        xs_ready, bc_ready = signal("xs_ready"), signal("bc_ready", 2)
        z_ready, gate_ready = signal("z_ready", 4), signal("gate_ready")
        gate_step = signal("gate_step")
        dtx_ready = signal("dtx_ready")
        dta_ready, dte_ready = signal("dta_ready"), signal("dte_ready")
        da_log_ready, dA_ready = signal("da_log_ready"), signal("dA_ready")
        dA_rows_ready, dA_T_ready = signal("dA_rows_ready"), signal("dA_T_ready", 2)
        decay_ready, L_ready = signal("decay_ready", TILES), signal("L_ready", TILES)
        BT_ready = signal("BT_ready")
        xdt_ready, to_end_ready, xend_ready = signal("xdt_ready", 2), signal("to_end_ready"), signal("xend_ready")
        M_ready = signal("M_ready", TILES)
        state_ready, stateT_ready = signal("state_ready", TILES - 1), signal("stateT_ready", 2)
        dx_ready = signal("dx_ready")
        yo_ready, yo_dx_ready, y_ready = (signal(n, 2) for n in ("yo_ready", "yo_dx_ready", "y_ready"))
        y2_ready, sq_ready = signal("y2_ready", 2), signal("sq_ready", 2)
        ms_ready, y_rstd_ready = signal("ms_ready"), signal("y_rstd_ready")
        y_rows_ready, y_T_ready = signal("y_rows_ready"), signal("y_T_ready")
        y_b_ready = signal("y_b_ready", 2)
        pooled_ready, hdn_ready, tha_ready = signal("pooled_ready", 2), signal("hdn_ready"), signal("tha_ready")
        fin_ready = signal("fin_ready", 2)
        out_sent = [signal(f"out_sent{n}", 16) for n in range(2)]
        ln_dve = Chain(ctx.enter_context(nc.semaphore("ln_dve")), 2)
        mamba_dve = Chain(ctx.enter_context(nc.semaphore("mamba_dve")), 18)

        bank_read = {"V0": (v_ready, 1), "V1": (v_ready, 2),
                     "X1T0": (ln_stats, 1), "X1T1": (ln_stats, 2),
                     "LnT": (ln_T_ready, 1), "LnB0": (u_ready, 1), "LnB1": (u_ready, 2),
                     "InX0": (raw_x_ready, 1), "InX1": (raw_x_ready, 2), "Dt": (dtx_ready, 1),
                     "InBC0": (raw_bc_ready, 1), "InBC1": (raw_bc_ready, 2), "InZ0": (z_ready, 2),
                     "InZ1": (z_ready, 4), "DAT": (dA_T_ready, 2), "Decay0": (decay_ready, 4),
                     "Decay1": (decay_ready, 8), "XsT0": (xdt_ready, 1), "XsT1": (xdt_ready, 2),
                     "BT": (BT_ready, 1), "G0": (M_ready, 4), "G1": (M_ready, 8), "U": (state_ready, 7),
                     "StT0": (stateT_ready, 1), "StT1": (stateT_ready, 2), "Yo0": (yo_ready, 1),
                     "Yo1": (yo_ready, 2), "Y0": (y_ready, 1), "Y1": (y_ready, 2), "Ss": (ms_ready, 1),
                     "YrT": (y_T_ready, 1), "YrB0": (y_b_ready, 1), "YrB1": (y_b_ready, 2),
                     "Out0": (pooled_ready, 1), "Out1": (pooled_ready, 2), "SeA": (hdn_ready, 1),
                     "SeB": (tha_ready, 1)}
        for i in range(TILES):
            bank_read[f"L{i}"] = (L_ready, i + 1)
        for i in range(2 * TILES):
            bank_read[f"T{i}"] = (pT_ready, i + 1)

        def fill(pe, t, uses, banks, memory, name, beside):
            kind = parse(name)[0]
            iteration = t + batches_behind(kind)
            before, ago = previous_use(uses, banks, name, iteration)
            if before is not None:
                signal, k = bank_read[before]
                wait(pe, signal, iteration - ago - batches_behind(parse(before)[0]), k, beside)
            return memory[uses[phase(iteration)].index(name) % banks], filled[kind].sem

        def turn_fill(pe, t, name, beside=None):
            return fill(pe, t, TURN_USES, 2, turn, name, beside)

        def mamba_fill(pe, t, name, beside=None):
            return fill(pe, t, MAMBA_USES, 3, mb, name, beside)

        def take(eng, t, uses, banks, memory, name):
            kind, k = parse(name)
            wait(eng, filled[kind], t, k + 1)
            return memory[uses[phase(t + batches_behind(kind))].index(name) % banks]

        def turn_take(eng, t, name):
            return take(eng, t, TURN_USES, 2, turn, name)

        def mamba_take(eng, t, name):
            return take(eng, t, MAMBA_USES, 3, mb, name)

        def run_streams(eng, attention, mamba, prepare):
            def iteration(t):
                for step in ORDERS[phase(t)]:
                    kind, k = parse(step)
                    (attention if kind in ATTENTION else mamba)(t - batches_behind(kind), kind, k)
                    if phase(t) == 0 and step in PREPARE:
                        prepare(PREPARE.index(step))

            iteration(0)
            iteration(1)
            with eng.Fori(2, BATCH) as t:
                iteration(t)
            iteration(BATCH)

        block = ctx.enter_context(nc.Block())

        @block.sync
        def _(sp):
            sp.dma_start(x_all[:, 0:TOKENS], x_d[0]).then_inc(x_in[0].sem, 16)
            sp.dma_start(wqkv[:, :, :], qkv_w.rearrange("(k o) c -> o k c", k=3)).then_inc(attn_w_in.sem, 16)
            sp.dma_start(wp[:, :], proj_w).then_inc(attn_w_in.sem, 16)
            for b in range(1, BATCH):
                sp.dma_start(x_all[:, b * TOKENS:(b + 1) * TOKENS], x_d[b]).then_inc(x_in[b].sem, 16)
            for k in range(3):
                sp.dma_start(win[:, k, :], in_w[k * P:(k + 1) * P, :]).then_inc(mamba_w_in.sem, 16)
            sp.dma_start(win[0:HEADS, 3, :], in_w[3 * P:INPROJ, :]).then_inc(mamba_w_in.sem, 16)
            sp.dma_start(wout[:, :], out_w).then_inc(mamba_w_in.sem, 16)
            sp.dma_start(wse1[:, :], se1_w).then_inc(mamba_w_in.sem, 16)
            sp.dma_start(wse2[:, :], se2_w).then_inc(mamba_w_in.sem, 16)

            for c, v in ((NG, norm_g), (NB, norm_b), (RMSW, rms_w), (SE2B, se2_b)):
                sp.dma_start(col[:, c:c + 1], v.rearrange("(p a) -> p a", a=1)).then_inc(mamba_w_in.sem, 16)
            sp.dma_start(col[:, DP:DP + 1],
                          Dp.rearrange("(h a) -> h a", a=1).broadcast_to([HEADS, HEADDIM])
                          ).then_inc(mamba_w_in.sem, 16)
            sp.dma_start(se1b[:, :], se1_b.rearrange("(p a) -> p a", a=1)).then_inc(mamba_w_in.sem, 16)
            for k in range(2):
                sp.dma_start(conv[:, k, 0:TAPS], conv_w[k * P:(k + 1) * P, :]).then_inc(mamba_w_in.sem, 16)
                sp.dma_start(conv[:, k, TAPS:TAPS + 1],
                              conv_b[k * P:(k + 1) * P].rearrange("(p a) -> p a", a=1)
                              ).then_inc(mamba_w_in.sem, 16)
            sp.dma_start(dtb_in[:, :], dt_bias.rearrange("(a h) -> a h", a=1).broadcast_to([P, HEADS])
                          ).then_inc(mamba_w_in.sem, 16)
            sp.dma_start(alog[:, :], A_log.rearrange("(a h) -> a h", a=1).broadcast_to([P, HEADS])
                          ).then_inc(mamba_w_in.sem, 16)

            def store(t):
                for n in range(2):
                    half = slice(n * HALF, (n + 1) * HALF)
                    wait(sp, fin_ready, t, n + 1)
                    sp.dma_start(out_d[bass.ds(t, 1)].rearrange("b c n -> (b c) n")[:, half], fin[:, half]
                                 ).then_inc(out_sent[n].sem, 16)

            with sp.Fori(0, BATCH) as t:
                store(t)
            for n in range(2):
                sp.wait_ge(out_sent[n].sem, 16 * BATCH)

        @block.gpsimd
        def _(pool):
            pool.memset(ident[:, :], 0.0).then_inc(pool_step.sem, 1)
            pool.memset(group_avg[:, :], 1.0 / (P // GROUPS)).then_inc(pool_step.sem, 1)
            pool.wait_ge(pool_step.sem, 2)
            pool.affine_select(out=ident[:, :], in_=ident[:, :], compare_op=ALU.not_equal, fill=1.0, base=0,
                               pattern=[[-1, P]], channel_multiplier=1).then_inc(consts_done.sem, 1)
            width = P // GROUPS
            view = group_avg[:, :].rearrange("p (g r) -> p g r", g=GROUPS)
            pool.affine_select(out=view, in_=view, compare_op=ALU.is_ge, fill=0.0, base=0,
                               pattern=[[-width, GROUPS], [0, width]], channel_multiplier=1
                               ).then_inc(pool_step.sem, 1)
            pool.wait_ge(pool_step.sem, 3)
            pool.affine_select(out=view, in_=view, compare_op=ALU.is_ge, fill=0.0, base=width - 1,
                               pattern=[[width, GROUPS], [0, width]], channel_multiplier=-1
                               ).then_inc(consts_done.sem, 1)
            pool.memset(zeros[:, :], 0.0).then_inc(consts_done.sem, 1)
            pool.memset(ones[:, :], 1.0).then_inc(consts_done.sem, 1)
            pool.memset(past_first[:, 1:P], 1.0).then_inc(consts_done.sem, 1)
            pool.memset(past_first[:, 0:1], 0.0).then_inc(consts_done.sem, 1)
            pool.memset(neg_half[:, :], -0.5).then_inc(consts_done.sem, 1)
            pool.memset(ln_rows[:, :, :], 0.0).then_inc(consts_done.sem, 1)
            pool.memset(y_rows[:, :, :], 0.0).then_inc(consts_done.sem, 1)
            pool.memset(raw[:, :, 0:PAD], 0.0).then_inc(consts_done.sem, 1)
            pool.wait_ge(consts_done.sem, 7)
            def group_norm_pow(n, b0, b1):
                pool.wait_ge(gn_step.sem, 3 * n + 3)
                pool.tensor_tensor(gn_rstd[:, b0:b1], gn_ve[:, b0:b1], neg_half[:, b0:b1], ALU.pow
                                   ).then_inc(gn_pow.sem, 1)

            group_norm_pow(0, 0, 1)

            def attention(t, kind, n):
                if kind == "scale":
                    wait(pool, inv_ready, t, n + 1, pool_passed)
                    pool.tensor_scalar(probs[:, n % 2, :], probs[:, n % 2, :], inv[:, n:n + 1], 1.0,
                                       ALU.mult, ALU.mult).then_inc(scaled.sem, 1)

            def prepare(n):
                if n == 4:
                    group_norm_pow(1, 1, BATCH)

            def mamba(t, kind, n):
                half = slice(n * HALF, (n + 1) * HALF)
                if kind == "ln_pow":
                    wait(pool, ln_ve_ready, t)
                    wait(pool, ln_rows_ready, t - 1)
                    pool.tensor_tensor(ln_rstd[:, :], ln_ve[:, :], neg_half[:, :], ALU.pow
                                       ).then_inc(ln_rstd_ready.sem, 1)
                elif kind == "gate" and n == 0:
                    wait(pool, z_ready, t, 4)
                    wait(pool, y2_ready, t - 1, 2)
                    pool.tensor_tensor(gate[:, :], thz[:, :], zv[:, :], ALU.mult).then_inc(gate_step.sem, 1)
                elif kind == "gate":
                    wait(pool, gate_step, t)
                    pool.tensor_tensor(gate[:, :], gate[:, :], zv[:, :], ALU.add).then_inc(gate_ready.sem, 1)
                elif kind == "xend":
                    wait(pool, xdt_ready, t, 2)
                    wait(pool, to_end_ready, t)
                    pool.tensor_tensor(xend[:, :, :], xdt[:, :, :],
                                       to_end[:, :].unsqueeze(2).broadcast_to([P, N32, HEADDIM]), ALU.mult
                                       ).then_inc(xend_ready.sem, 1)
                elif kind == "dx":
                    wait(pool, xs_ready, t)
                    wait(pool, y_ready, t - 1, 2, pool_passed)
                    pool.tensor_scalar(yo[:, 0:P], xs[:, 0:P], col[:, DP:DP + 1], 0.0, ALU.mult, ALU.add)
                    pool.tensor_scalar(dx[:, P:TOKENS], xs[:, P:TOKENS], col[:, DP:DP + 1], 0.0, ALU.mult, ALU.add
                                       ).then_inc(dx_ready.sem, 1)
                elif kind == "yo_dx":
                    part = slice(P, HALF) if n == 0 else half
                    wait(pool, dx_ready, t)
                    wait(pool, yo_ready, t, n + 1)
                    pool.tensor_tensor(yo[:, part], yo[:, part], dx[:, part], ALU.add).then_inc(yo_dx_ready.sem, 1)
                elif kind == "y_pow":
                    wait(pool, ms_ready, t)
                    wait(pool, y_rows_ready, t - 1)
                    pool.tensor_tensor(y_rstd[:, :], ms[:, :], neg_half[:, :], ALU.pow
                                       ).then_inc(y_rstd_ready.sem, 1)

            run_streams(pool, attention, mamba, prepare)

        @block.scalar
        def _(act):
            vectors = ((GNW, gn_w), (GNB, gn_b), (QB, qkv_b[0:P]), (VB, qkv_b[2 * P:3 * P]), (PB, proj_b))
            for c, v in vectors:
                act.dma_start(col[:, c:c + 1], v.rearrange("(p a) -> p a", a=1)).then_inc(attn_w_in.sem, 16)
            act.wait_ge(consts_done.sem, 10)
            act.activation(tha[:, :], ones[:, :], ACT.Exp)

            def attention(t, kind, n):
                half = slice(n * HALF, (n + 1) * HALF)
                if kind == "h":
                    act.wait_ge(gn_ready.sem, 1 if isinstance(t, int) and t == 0 else 2)
                    wait(act, h_split, t - 1, 2)
                    act.activation(h32[:, :], x_all[:, bass.ds(t * TOKENS, TOKENS)], ACT.Identity,
                                   bias=gn_bias[:, bass.ds(t, 1)], scale=gn_scale[:, bass.ds(t, 1)]
                                   ).then_inc(h_ready.sem, 1)
                elif kind == "q_hi":
                    wait(act, scores_filled, t, 1)
                    act.activation(q_hi[:, half], scores[:, half], ACT.Identity, bias=col[:, QA:QA + 1]
                                   ).then_inc(q_hi_ready.sem, 1)
                elif kind == "v":
                    bank = turn_take(act, t, f"V{n}")
                    act.activation(values[:, 4 * n:4 * n + 4, :], bank[:, :].rearrange("p (a b) -> p a b", a=4),
                                   ACT.Copy).then_inc(v_ready.sem, 1)
                elif kind == "exp":
                    i, h = divmod(n, 2)
                    half = slice(h * HALF, (h + 1) * HALF)
                    wait(act, max_ready, t, i + 1)
                    wait(act, filled["T"], t, n - 3)
                    act.activation(probs[:, i % 2, half], scores[:, half], ACT.Exp, bias=neg_max[:, i:i + 1],
                                   accum_out=row_sum[:, h, i:i + 1]).then_inc(exp_done.sem, 1)
                elif kind == "pT":
                    i, h = divmod(n, 2)
                    g, i2 = divmod(i, 2)
                    if n % 4 == 0:
                        wait(act, pv_done, t, g - 1)
                    bank = turn_take(act, t, f"T{n}")
                    act.activation(pT[:, g % 2, 4 * h:4 * h + 4, i2 * P:(i2 + 1) * P],
                                   bank[:, :].rearrange("p (a b) -> p a b", a=4), ACT.Copy
                                   ).then_inc(pT_ready.sem, 1)

            def mamba(t, kind, n):
                half = slice(n * HALF, (n + 1) * HALF)
                if kind == "keep":
                    wait(act, x1_ready, t, n + 1, act_passed)
                    act.activation(x_all[:, bass.ds(t * TOKENS + n * HALF, HALF)], x1[:, half], ACT.Copy
                                   ).then_inc(x1_kept.sem, 1)
                elif kind in ("raw_x", "raw_bc"):
                    k, use, bias, ready, tap = ((0, "InX", BX, raw_x_ready, tap_x) if kind == "raw_x" else
                                                (1, "InBC", BBC, raw_bc_ready, tap_bc))
                    if n == 0:
                        wait(act, tap, t - 1, TAPS)
                    bank = mamba_take(act, t, f"{use}{n}")
                    act.activation(raw[:, k, PAD + n * HALF:PAD + (n + 1) * HALF], bank[:, :],
                                   ACT.Identity, bias=col[:, bias:bias + 1]).then_inc(ready.sem, 1)
                elif kind in ("conv_x", "conv_bc") and n == 0:
                    k, ready, tap, used = ((0, raw_x_ready, tap_x, (xs_ready, 1)) if kind == "conv_x" else
                                           (1, raw_bc_ready, tap_bc, (bc_ready, 2)))
                    wait(act, used[0], t - 1, used[1])
                    wait(act, ready, t, 2)
                    act.activation(pre[:, k, :], raw[:, k, 0:TOKENS], ACT.Identity, scale=conv[:, k, 0:1],
                                   bias=conv[:, k, TAPS:TAPS + 1]).then_inc(tap.sem, 1)
                elif kind == "z":
                    if n == 0:
                        wait(act, gate_ready, t - 1)
                    bank = mamba_take(act, t, f"InZ{n}")
                    act.activation(thz[:, half], bank[:, :], ACT.Tanh, bias=half_bz[:, :], scale=0.5
                                   ).then_inc(z_ready.sem, 1)
                    act.activation(zv[:, half], bank[:, :], ACT.Identity, bias=half_bz[:, :], scale=0.5
                                   ).then_inc(z_ready.sem, 1)
                elif kind == "sp_exp":
                    wait(act, dta_ready, t)
                    act.activation(dte[:, :], dta[:, :], ACT.Exp, scale=-1.0).then_inc(dte_ready.sem, 1)
                elif kind == "th_x":
                    wait(act, tap_x, t, TAPS)
                    act.activation(th[:, 0, :], pre[:, 0, :], ACT.Tanh).then_inc(th_x_ready.sem, 1)
                elif kind == "th_bc":
                    wait(act, tap_bc, t, TAPS)
                    act.activation(th[:, 1, :], pre[:, 1, :], ACT.Tanh).then_inc(th_bc_ready.sem, 1)
                elif kind == "dA":
                    wait(act, da_log_ready, t)
                    act.activation(dA[:, :], dtw[:, 4, :], ACT.Exp, scale=1.0 / A_SCALE
                                   ).then_inc(dA_ready.sem, 1)
                elif kind == "bt":
                    bank = mamba_take(act, t, "BT")
                    act.activation(BT[:, :, :], bank[:, :].rearrange("p (c n) -> p c n", c=TILES), ACT.Copy
                                   ).then_inc(BT_ready.sem, 1)
                elif kind == "st_T":
                    c0 = 1 if n == 0 else 0
                    bank = mamba_take(act, t, f"StT{n}")
                    act.activation(stateT[:, 4 * n + c0:4 * n + 4, :],
                                   bank[0:STATE, c0 * P:4 * P].rearrange("p (c n) -> p c n", n=P),
                                   ACT.Copy).then_inc(stateT_ready.sem, 1)
                elif kind == "sq":
                    wait(act, y2_ready, t, n + 1)
                    act.activation(sq[:, half], y2[:, half], ACT.Square).then_inc(sq_ready.sem, 1)
                elif kind == "y_b":
                    wait(act, pooled_ready, t - 1, n + 1)
                    bank = mamba_take(act, t, f"YrB{n}")
                    act.activation(y_b[:, half], bank[:, :], ACT.Copy).then_inc(y_b_ready.sem, 1)
                elif kind == "hdn":
                    bank = mamba_take(act, t, "SeA")
                    act.activation(hdn[:, :], bank[0:SE, 0:1], ACT.Relu, bias=se1b[:, :], scale=1.0 / TOKENS
                                   ).then_inc(hdn_ready.sem, 1)
                elif kind == "tha":
                    bank = mamba_take(act, t, "SeB")
                    act.activation(tha[:, :], bank[:, 0:1], ACT.Tanh, bias=half_se2b[:, :], scale=0.5
                                   ).then_inc(tha_ready.sem, 1)

            def prepare(n):
                if n == 2:
                    act.wait_ge(alog_clamped.sem, 1)
                    act.activation(a_exp[:, :], alog[:, :], ACT.Exp).then_inc(a_exp_ready.sem, 1)

            run_streams(act, attention, mamba, prepare)

        @block.vector
        def _(dve):
            V = nc.vector
            prep = [0]

            def step_done(ins):
                prep[0] += 1
                ins.then_inc(dve_prep.sem, 1)
                dve.wait_ge(dve_prep.sem, prep[0])

            dve.wait_ge(consts_done.sem, 10)
            for h in range(HEADS):
                V.tensor_copy(ident4[:, h, :], ident[:, :])
            V.tensor_scalar(center[:, :], ident[:, :], 1.0 / P, None, ALU.subtract)
            step_done(V.tensor_tensor(pick_row[:, :], ident[0:64, 0:32], ident[0:64, 32:64], ALU.add))
            step_done(V.tensor_copy(
                pick_head[:, :, :].rearrange("k c (h p) -> k (c h) p", h=HEADS),
                pick_row[:, :].bitcast(F32).unsqueeze(2).broadcast_to([64, 32, HEADDIM])))

            def gn_stats(b0, b1):
                for b in range(b0, b1):
                    dve.wait_ge(x_in[b].sem, 16)
                    for k in range(2):
                        ins = V.bn_stats(gn_raw[:, b, k, :], x_all[:, b * TOKENS + k * HALF:b * TOKENS + (k + 1) * HALF])
                step_done(ins)
                for b in range(b0, b1):
                    ins = V.bn_aggr(gn_mv[:, b, :], gn_raw[:, b, :, :])
                ins.then_inc(gn_step.sem, 1)

            def gn_spread(n, b0, b1):
                dve.wait_ge(gn_mm.sem, 2 * n + 1)
                step_done(V.tensor_copy(gn_mean[:, b0:b1], mb[2][:, b0:b1]))
                step_done(V.tensor_tensor(gn_dev[:, b0:b1], gn_mv[:, b0:b1, 0], gn_mean[:, b0:b1], ALU.subtract))
                step_done(V.tensor_tensor(gn_dev[:, b0:b1], gn_dev[:, b0:b1], gn_dev[:, b0:b1], ALU.mult))
                V.tensor_tensor(gn_dev[:, b0:b1], gn_dev[:, b0:b1], gn_mv[:, b0:b1, 1], ALU.add
                                ).then_inc(gn_step.sem, 1)

            def gn_variance(n, b0, b1):
                dve.wait_ge(gn_mm.sem, 2 * n + 2)
                V.tensor_scalar(gn_ve[:, b0:b1], mb[2][:, b0:b1], EPS, None, ALU.add).then_inc(gn_step.sem, 1)

            def gn_affine(n, b0, b1):
                dve.wait_ge(gn_pow.sem, n + 1)
                step_done(V.tensor_scalar(gn_scale[:, b0:b1], gn_rstd[:, b0:b1], col[:, GNW:GNW + 1], None, ALU.mult))
                step_done(V.tensor_tensor(gn_bias[:, b0:b1], gn_mean[:, b0:b1], gn_scale[:, b0:b1], ALU.mult))
                V.tensor_scalar(gn_bias[:, b0:b1], gn_bias[:, b0:b1], -1.0, col[:, GNB:GNB + 1], ALU.mult, ALU.add
                                ).then_inc(gn_ready.sem, 1)

            gn_stats(0, 1)
            gn_spread(0, 0, 1)
            gn_variance(0, 0, 1)
            dve.wait_ge(attn_w_in.sem, 16 * 7)
            dve.wait_ge(prep_mm.sem, 1)
            step_done(V.tensor_scalar(wpT[:, :], turn[0][:, 0:P], 1.0, None, ALU.mult))
            step_done(V.tensor_scalar(key_query_hi[:, :], turn[0][:, P:2 * P], SCORE_SCALE, None, ALU.mult))
            V.scalar_tensor_tensor(key_query_lo[:, :], turn[0][:, P:2 * P], SCORE_SCALE,
                                   key_query_hi[:, :].bitcast(F32), ALU.mult, ALU.subtract)
            V.tensor_scalar(col[:, QA:QA + 1], turn[0][:, 2 * P:2 * P + 1], SCORE_SCALE, None, ALU.mult
                            ).then_inc(prep_evac.sem, 1)
            gn_affine(0, 0, 1)
            dve.wait_ge(prep_mm.sem, 2)
            step_done(V.tensor_copy(value_proj_hi[:, :], turn[1][:, 0:P]))
            V.tensor_tensor(value_proj_lo[:, :], turn[1][:, 0:P], value_proj_hi[:, :].bitcast(F32), ALU.subtract)
            V.tensor_tensor(col[:, OB:OB + 1], turn[1][:, P:P + 1], col[:, PB:PB + 1], ALU.add
                            ).then_inc(prep_evac.sem, 1)

            def attention(t, kind, n):
                half = slice(n * HALF, (n + 1) * HALF)
                if kind == "h_hi":
                    wait(dve, h_ready, t)
                    wait(dve, scores_filled, t - 1, len(SCORE_USES))
                    V.tensor_copy(h_hi[:, :], h32[:, :]).then_inc(h_split.sem, 1)
                elif kind == "h_lo":
                    wait(dve, h_split, t, 1)
                    V.tensor_tensor(h_lo[:, :], h32[:, :], h_hi[:, :].bitcast(F32), ALU.subtract
                                    ).then_inc(h_split.sem, 1)
                elif kind == "q_lo":
                    wait(dve, q_hi_ready, t, n + 1)
                    V.scalar_tensor_tensor(q_lo[:, half], scores[:, half], col[:, QA:QA + 1],
                                           q_hi[:, half].bitcast(F32), ALU.add, ALU.subtract
                                           ).then_inc(q_lo_ready.sem, 1)
                elif kind == "max":
                    wait(dve, scores_filled, t, 2 * n + 3)
                    V.tensor_reduce(neg_max[:, n:n + 1], scores[:, :], AX.X, ALU.max, negate=True
                                    ).then_inc(max_ready.sem, 1)
                elif kind == "sum":
                    wait(dve, exp_done, t, 2 * n + 2)
                    V.tensor_tensor(row_total[:, n:n + 1], row_sum[:, 0, n:n + 1], row_sum[:, 1, n:n + 1], ALU.add
                                    ).then_inc(summed.sem, 1)
                elif kind == "inv":
                    wait(dve, summed, t, n + 1)
                    V.reciprocal(inv[:, n:n + 1], row_total[:, n:n + 1]).then_inc(inv_ready.sem, 1)
                elif kind == "norm":
                    wait(dve, x1_kept, t - 1, 2)
                    wait(dve, pv_done, t, 2 * n + 2)
                    V.scalar_tensor_tensor(x1[:, half], attn_out[:, :], col[:, OB:OB + 1],
                                           x_all[:, bass.ds(t * TOKENS + n * HALF, HALF)], ALU.add, ALU.add
                                           ).then_inc(x1_ready.sem, 1)

            def rows_split(chain, t, rows, value, ready):
                n = value.shape[1]
                chain.done(V.tensor_copy(rows[:, 0, 0:n].bitcast(F32R), value))
                chain.before(dve, t)
                V.tensor_tensor(rows[:, 1, 0:n], value, rows[:, 0, 0:n], ALU.subtract).then_inc(ready.sem, 1)

            def softplus(t, n):
                e, s, s2, acc = dtw[:, 0, :], dtw[:, 1, :], dtw[:, 2, :], dtw[:, 3, :]
                by_head = lambda a: a.rearrange("p (c h) -> p c h", h=HEADS)
                if n == 0:
                    return V.tensor_scalar(e, dte[:, :], 2.0, None, ALU.add)
                if n == 1:
                    return V.reciprocal(s, e)
                if n == 2:
                    return V.tensor_tensor(s, s, dte[:, :], ALU.mult)
                if n == 3:
                    return V.tensor_tensor(s2, s, s, ALU.mult)
                if n == 4:
                    return V.tensor_scalar(acc, s2, 1.0 / 15, None, ALU.mult)
                if n <= 10:
                    return V.scalar_tensor_tensor(acc, acc, 1.0 / (13 - 2 * (n - 5)), s2, ALU.add, ALU.mult)
                if n == 11:
                    return V.scalar_tensor_tensor(acc, acc, 1.0, s, ALU.add, ALU.mult)
                if n == 12:
                    return V.tensor_scalar(e, dtx[:, :], 0.0, None, ALU.max)
                if n == 13:
                    return V.scalar_tensor_tensor(dt[:, :], acc, 2.0, e, ALU.mult, ALU.add)
                if n == 14:
                    return V.tensor_tensor(by_head(dtw[:, 4, :]), by_head(dt[:, :]),
                                           a_neg[:, :].unsqueeze(1).broadcast_to([P, TILES, HEADS]), ALU.mult)
                return V.tensor_scalar(dtw[:, 4, :], dtw[:, 4, :], DA_LOG_MIN * A_SCALE, None, ALU.max)

            def mamba(t, kind, n):
                half = slice(n * HALF, (n + 1) * HALF)
                if kind == "stats":
                    bank = mamba_take(dve, t, f"X1T{n}")
                    for c in range(4):
                        ins = V.bn_stats(ln_raw[:, 4 * n + c, :], bank[:, c * P:(c + 1) * P])
                    ins.then_inc(ln_stats.sem, 1)
                elif kind == "ln_ve":
                    ln_dve.start()
                    wait(dve, ln_stats, t, 2, dve_passed)
                    for c in range(TILES):
                        ins = V.bn_aggr(ln_mv[:, c, :], ln_raw[:, c, :])
                    ln_dve.done(ins)
                    ln_dve.before(dve, t)
                    V.tensor_scalar(ln_ve[:, :], ln_mv[:, :, 1], EPS, None, ALU.add).then_inc(ln_ve_ready.sem, 1)
                elif kind == "ln_rows":
                    wait(dve, ln_rstd_ready, t)
                    rows_split(ln_dve, t, ln_rows, ln_rstd[:, :], ln_rows_ready)
                    ln_dve.end()
                elif kind == "ln_T":
                    bank = mamba_take(dve, t, "LnT")
                    V.tensor_copy(ln_T[:, :], bank[0:64, 0:P]).then_inc(ln_T_ready.sem, 1)
                elif kind == "u":
                    bank = mamba_take(dve, t, f"LnB{n}")
                    V.tensor_tensor(u[:, half], bank[:, :], x1[:, half], ALU.mult).then_inc(u_ready.sem, 1)
                elif kind == "dt_x":
                    bank = mamba_take(dve, t, "Dt")
                    V.tensor_tensor(dtx[:, :].rearrange("p (c h) -> p c h", h=HEADS),
                                    bank[:, 0:N32].rearrange("p (c h) -> p c h", h=HEADS),
                                    dtb[:, :].unsqueeze(1).broadcast_to([P, TILES, HEADS]), ALU.add
                                    ).then_inc(dtx_ready.sem, 1)
                    wait(dve, dtx_ready, t)
                    V.scalar_tensor_tensor(dta[:, :], dtx[:, :], -1.0, dtx[:, :], ALU.mult, ALU.max
                                           ).then_inc(dta_ready.sem, 1)
                elif kind in ("conv_x", "conv_bc") and n > 0:
                    k, tap = (0, tap_x) if kind == "conv_x" else (1, tap_bc)
                    wait(dve, tap, t, n)
                    V.scalar_tensor_tensor(pre[:, k, :], raw[:, k, n:n + TOKENS], conv[:, k, n:n + 1],
                                           pre[:, k, :], ALU.mult, ALU.add).then_inc(tap.sem, 1)
                elif kind == "sp":
                    if n == 0:
                        mamba_dve.start()
                        wait(dve, dte_ready, t)
                    else:
                        mamba_dve.before(dve, t)
                    if n < 15:
                        mamba_dve.done(softplus(t, n))
                    else:
                        softplus(t, n).then_inc(da_log_ready.sem, 1)
                elif kind == "xs":
                    wait(dve, th_x_ready, t)
                    V.scalar_tensor_tensor(xs[:, :], th[:, 0, :], 1.0, pre[:, 0, :], ALU.add, ALU.mult
                                           ).then_inc(xs_ready.sem, 1)
                elif kind == "dA_rows":
                    wait(dve, dA_ready, t)
                    rows_split(mamba_dve, t, dA_rows, dA[:, :], dA_rows_ready)
                elif kind == "dA_T":
                    bank = mamba_take(dve, t, "DAT")
                    V.tensor_copy(dA_T[:, :], bank[0:64, 0:P]).then_inc(dA_T_ready.sem, 1)
                    V.tensor_tensor(dA_Tz[:, :], bank[0:64, 0:P], past_first[:, :], ALU.mult
                                    ).then_inc(dA_T_ready.sem, 1)
                elif kind == "silu_b":
                    wait(dve, th_bc_ready, t)
                    V.scalar_tensor_tensor(B[:, :], th[0:STATE, 1, :], 1.0, pre[0:STATE, 1, :], ALU.add, ALU.mult
                                           ).then_inc(bc_ready.sem, 1)
                elif kind == "silu_c":
                    wait(dve, th_bc_ready, t)
                    V.scalar_tensor_tensor(C[:, :], th[STATE:P, 1, :], 1.0, pre[STATE:P, 1, :], ALU.add, ALU.mult
                                           ).then_inc(bc_ready.sem, 1)
                elif kind == "decay":
                    bank = mamba_take(dve, t, f"Decay{n}")
                    for c in range(4):
                        V.tensor_tensor_scan(decay_in[:, (4 * n + c) * P:(4 * n + c + 1) * P],
                                             bank[:, c * P:(c + 1) * P], zeros[:, :], 1.0, ALU.mult, ALU.add
                                             ).then_inc(decay_ready.sem, 1)
                elif kind == "xdt":
                    bank = mamba_take(dve, t, f"XsT{n}")
                    part = slice(16 * n, 16 * n + 16)
                    V.tensor_tensor(xdt[:, part, :], bank[:, :].rearrange("p (a b) -> p a b", b=HEADDIM),
                                    dt[:, part].unsqueeze(2).broadcast_to([P, 16, HEADDIM]), ALU.mult
                                    ).then_inc(xdt_ready.sem, 1)
                elif kind == "l":
                    bank = mamba_take(dve, t, f"L{n}")
                    V.tensor_tensor_scan(L[:, 4 * n:4 * n + 4, :].rearrange("p a b -> p (a b)"), bank[:, :],
                                         ident4[:, :, :].rearrange("p a b -> p (a b)"), 0.0, ALU.mult, ALU.add
                                         ).then_inc(L_ready.sem, 1)
                elif kind == "to_end":
                    wait(dve, L_ready, t, TILES)
                    wait(dve, xend_ready, t - 1)
                    V.tensor_copy(to_end[:, :], L[:, :, P - 1]).then_inc(to_end_ready.sem, 1)
                elif kind == "m":
                    bank = mamba_take(dve, t, f"G{n // 4}")
                    wait(dve, to_end_ready, t)
                    V.tensor_tensor(M[:, 4 * n:4 * n + 4, :], L[:, 4 * n:4 * n + 4, :],
                                    bank[:, (n % 4) * P:(n % 4 + 1) * P].unsqueeze(1).broadcast_to([P, HEADS, P]),
                                    ALU.mult).then_inc(M_ready.sem, 1)
                elif kind == "st" and n == 0:
                    bank = mamba_take(dve, t, "U")
                    V.tensor_copy(state[:, 1, :], bank[:, 0:STATE]).then_inc(state_ready.sem, 1)
                elif kind == "st":
                    bank = mamba_take(dve, t, "U")
                    wait(dve, decay_ready, t, n + 1)
                    wait(dve, state_ready, t, n)
                    V.scalar_tensor_tensor(state[:, n + 1, :], state[:, n, :],
                                           decay_in[:, (n + 1) * P - 1:(n + 1) * P],
                                           bank[:, n * STATE:(n + 1) * STATE], ALU.mult, ALU.add
                                           ).then_inc(state_ready.sem, 1)
                elif kind == "yo":
                    part = slice(P, HALF) if n == 0 else slice(HALF, TOKENS)
                    bank = mamba_take(dve, t, f"Yo{n}")
                    wait(dve, decay_ready, t, TILES)
                    V.tensor_tensor(yo[:, part], bank[:, P if n == 0 else 0:HALF], decay_in[:, part], ALU.mult
                                    ).then_inc(yo_ready.sem, 1)
                elif kind == "y":
                    bank = mamba_take(dve, t, f"Y{n}")
                    wait(dve, yo_dx_ready, t, n + 1)
                    wait(dve, out_sent[n], t - 1, 16)
                    V.tensor_tensor(y[:, half], bank[:, :], yo[:, half], ALU.add).then_inc(y_ready.sem, 1)
                elif kind == "g":
                    wait(dve, gate_ready, t)
                    wait(dve, y_ready, t, n + 1)
                    V.tensor_tensor(y2[:, half], y[:, half], gate[:, half], ALU.mult).then_inc(y2_ready.sem, 1)
                elif kind == "ms":
                    bank = mamba_take(dve, t, "Ss")
                    V.tensor_scalar(ms[:, :], bank[:, 0:TILES], 1.0 / P, EPS, ALU.mult, ALU.add
                                    ).then_inc(ms_ready.sem, 1)
                elif kind == "y_rows":
                    wait(dve, y_rstd_ready, t)
                    rows_split(mamba_dve, t, y_rows, y_rstd[:, :], y_rows_ready)
                elif kind == "y_T":
                    bank = mamba_take(dve, t, "YrT")
                    V.tensor_copy(y_T[:, :], bank[0:64, 0:P]).then_inc(y_T_ready.sem, 1)
                elif kind == "o":
                    wait(dve, y_b_ready, t, n + 1)
                    bank = mamba_take(dve, t, f"Out{n}")
                    V.tensor_tensor_reduce(out=o_img[:, half], in0=bank[:, :], in1=y_b[:, half], scale=1.0,
                                           scalar=0.0, op0=ALU.mult, op1=ALU.add,
                                           accum_out=pooled[:, n:n + 1]).then_inc(pooled_ready.sem, 1)
                elif kind == "att":
                    wait(dve, tha_ready, t)
                    mamba_dve.done(V.tensor_scalar(att[:, :], tha[:, :], 1.0, 0.5, ALU.add, ALU.mult))
                elif kind == "fin":
                    mamba_dve.before(dve, t)
                    wait(dve, x1_kept, t, n + 1)
                    V.scalar_tensor_tensor(fin[:, half], o_img[:, half], att[:, :],
                                           x_all[:, bass.ds(t * TOKENS + n * HALF, HALF)], ALU.mult, ALU.add
                                           ).then_inc(fin_ready.sem, 1)
                    if n == 1:
                        mamba_dve.end()

            def prepare(n):
                if n == 0:
                    gn_stats(1, BATCH)
                if n == 1:
                    dve.wait_ge(mamba_w_in.sem, 16 * 19)
                    V.tensor_scalar(alog[:, :], alog[:, :], A_LOG_MAX, None, ALU.min).then_inc(alog_clamped.sem, 1)
                    V.tensor_scalar(conv[:, :, :], conv[:, :, :], 0.5, None, ALU.mult)
                    V.tensor_scalar(half_se2b[:, :], col[:, SE2B:SE2B + 1], 0.5, None, ALU.mult)
                    dve.wait_ge(prep_mm.sem, 3)
                    V.tensor_copy(winT[:, :], mb[0][:, 0:INPROJ])
                    V.tensor_scalar(winTg[:, :], mb[0][:, 0:INPROJ], col[:, NG:NG + 1], None, ALU.mult
                                    ).then_inc(prep_evac.sem, 1)
                    dve.wait_ge(prep_mm.sem, 4)
                    V.tensor_scalar(woutT[:, :], mb[1][:, 0:P], col[:, RMSW:RMSW + 1], None, ALU.mult)
                    V.tensor_copy(se1T[:, :], mb[1][:, P:P + SE])
                    V.tensor_copy(se2T[:, :], mb[1][0:SE, 2 * P:3 * P]).then_inc(prep_evac.sem, 1)
                if n == 2:
                    gn_spread(1, 1, BATCH)
                if n == 4:
                    gn_variance(1, 1, BATCH)
                if n == 5:
                    gn_affine(1, 1, BATCH)
                if n == 3:
                    dve.wait_ge(a_exp_ready.sem, 1)
                    V.tensor_scalar(a_neg[:, :], a_exp[:, :], -A_SCALE, None, ALU.mult)
                    dve.wait_ge(prep_mm.sem, 5)
                    V.tensor_copy(winC[:, :], mb[0][:, 0:INPROJ])
                    V.tensor_tensor(dtb[:, :], mb[0][:, 400:400 + HEADS], dtb_in[:, :], ALU.add)
                    V.tensor_scalar(half_bz[:, :], mb[0][:, 408:409], 0.5, None, ALU.mult)
                    V.tensor_copy(col[:, BX:BBC + 1], mb[0][:, 410:412]).then_inc(prep_evac.sem, 1)

            run_streams(dve, attention, mamba, prepare)

        @block.tensor
        def _(pe):
            T = nc.tensor

            def mm(o, w, v, start=True, stop=True):
                return T.matmul(o, w, v, start=start, stop=stop)

            def mm3(o, w_hi, w_lo, v_hi, v_lo, start=True, stop=True):
                mm(o, w_hi, v_hi, start, False)
                mm(o, w_hi, v_lo, False, False)
                return mm(o, w_lo, v_hi, False, stop)

            pe.wait_ge(consts_done.sem, 10)

            def group_mean(n, b0, b1, step, value):
                pe.wait_ge(gn_step.sem, 3 * n + step)
                mm(mb[2][:, b0:b1], group_avg[:, :], value).then_inc(gn_mm.sem, 1)

            group_mean(0, 0, 1, 1, gn_mv[:, 0:1, 0])
            group_mean(0, 0, 1, 2, gn_dev[:, 0:1])
            pe.wait_ge(attn_w_in.sem, 16 * 7)
            T.transpose(turn[0][:, 0:P], wp[:, :], ident[:, :])
            mm(turn[0][:, P:2 * P], wqkv[:, 0, :], wqkv[:, 1, :])
            mm(turn[0][:, 2 * P:2 * P + 1], wqkv[:, 1, :], col[:, QB:QB + 1]).then_inc(prep_mm.sem, 1)

            pe.wait_ge(prep_evac.sem, 1)
            mm(turn[1][:, 0:P], wqkv[:, 2, :], wpT[:, :])
            mm(turn[1][:, P:P + 1], wpT[:, :], col[:, VB:VB + 1]).then_inc(prep_mm.sem, 1)
            pe.wait_ge(prep_evac.sem, 2)

            def prepare(n):
                if n == 0:
                    pe.wait_ge(mamba_w_in.sem, 16 * 19)
                    for k in range(3):
                        T.transpose(mb[0][:, k * P:(k + 1) * P], win[:, k, :], ident[:, :])
                    T.transpose(mb[0][:, 3 * P:INPROJ], win[0:HEADS, 3, :], ident[0:HEADS, 0:HEADS]
                                ).then_inc(prep_mm.sem, 1)
                    T.transpose(mb[1][:, 0:P], wout[:, :], ident[:, :])
                    T.transpose(mb[1][:, P:P + SE], wse1[:, :], ident[0:SE, 0:SE])
                    T.transpose(mb[1][0:SE, 2 * P:3 * P], wse2[:, :], ident[:, :]).then_inc(prep_mm.sem, 1)
                if n == 1:
                    group_mean(1, 1, BATCH, 1, gn_mv[:, 1:BATCH, 0])
                if n == 3:
                    group_mean(1, 1, BATCH, 2, gn_dev[:, 1:BATCH])
                if n == 2:
                    pe.wait_ge(prep_evac.sem, 4)
                    mm(mb[0][:, 0:INPROJ], center[:, :], winTg[:, :])
                    mm(mb[0][:, 400:400 + HEADS], col[:, NB:NB + 1].broadcast_to([P, P]), winT[:, 3 * P:INPROJ])
                    for k, at in ((0, 408), (1, 410), (2, 411)):
                        last = mm(mb[0][:, at:at + 1], winT[:, k * P:(k + 1) * P], col[:, NB:NB + 1])
                    last.then_inc(prep_mm.sem, 1)

            def pick(r):
                return pick_row[:, r:r + 1].broadcast_to([64, P])

            def tiles_of(n):
                return [(slice(c * P, (c + 1) * P), slice((4 * n + c) * P, (4 * n + c + 1) * P)) for c in range(4)]

            def rows_out(bank, rows):
                return T.transpose(bank[0:64, 0:P], rows[:, :, :].rearrange("p a b -> p (a b)"), ident[:, :])

            def attention(t, kind, n):
                if kind == "Q":
                    wait(pe, h_split, t, 2)
                    wait(pe, exp_done, t - 1, 2 * TILES)
                    for m in range(2):
                        half = slice(m * HALF, (m + 1) * HALF)
                        last = mm3(scores[:, half], key_query_hi[:, :], key_query_lo[:, :], h_hi[:, half], h_lo[:, half])
                    last.then_inc(scores_filled.sem, 1)
                elif kind == "V":
                    wait(pe, h_split, t, 2)
                    bank, filled = turn_fill(pe, t, f"V{n}")
                    for cols, tile in tiles_of(n):
                        last = mm3(bank[:, cols], h_hi[:, tile], h_lo[:, tile],
                                   value_proj_hi[:, :], value_proj_lo[:, :])
                    last.then_inc(filled, 1)
                elif kind == "S":
                    i, h = divmod(n, 2)
                    wait(pe, q_lo_ready, t, 2)
                    if n >= 2:
                        wait(pe, exp_done, t, n - 1)
                    tile, half = slice(i * P, (i + 1) * P), slice(h * HALF, (h + 1) * HALF)
                    mm3(scores[:, half], q_hi[:, tile], q_lo[:, tile], h_hi[:, half], h_lo[:, half]
                        ).then_inc(scores_filled.sem, 1)
                elif kind == "T":
                    wait(pe, scaled, t, n // 2 + 1)
                    bank, filled = turn_fill(pe, t, f"T{n}")
                    for cols, tile in tiles_of(n % 2):
                        last = T.transpose(bank[:, cols], probs[:, n // 2 % 2, tile], ident[:, :])
                    last.then_inc(filled, 1)
                elif kind == "PV":
                    g, part = divmod(n, 2)
                    wait(pe, pT_ready, t, 4 * g + 3 + part)
                    if part == 0:
                        wait(pe, v_ready, t, 2)
                        wait(pe, x1_ready, t, g // 2)
                    b = g % 2
                    for k in range(4 * part, 4 * part + 4):
                        last = mm(attn_out[:, b * 2 * P:(b + 1) * 2 * P], values[:, k, :], pT[:, b, k, :],
                                  k == 0, k == TILES - 1)
                    if part == 1:
                        last.then_inc(pv_done.sem, 1)

            def mamba(t, kind, n):
                half = slice(n * HALF, (n + 1) * HALF)
                if kind == "X1T":
                    wait(pe, x1_ready, t, n + 1)
                    bank, filled = mamba_fill(pe, t, f"X1T{n}")
                    for c in range(4):
                        last = T.transpose(bank[:, c * P:(c + 1) * P], x1[:, (4 * n + c) * P:(4 * n + c + 1) * P],
                                           ident[:, :])
                    last.then_inc(filled, 1)
                elif kind in ("LnT", "DAT", "YrT"):
                    rows, ready = {"LnT": (ln_rows, ln_rows_ready), "DAT": (dA_rows, dA_rows_ready),
                                   "YrT": (y_rows, y_rows_ready)}[kind]
                    wait(pe, ready, t)
                    bank, filled = mamba_fill(pe, t, kind, pe_passed)
                    rows_out(bank, rows).then_inc(filled, 1)
                elif kind in ("LnB", "YrB"):
                    row, ready = (ln_T, ln_T_ready) if kind == "LnB" else (y_T, y_T_ready)
                    wait(pe, ready, t)
                    bank, filled = mamba_fill(pe, t, f"{kind}{n}")
                    for c in range(4):
                        last = mm(bank[:, c * P:(c + 1) * P], pick(4 * n + c), row[:, :])
                    last.then_inc(filled, 1)
                elif kind in ("InX", "InBC", "InZ"):
                    k = {"InX": 1, "InBC": 2, "InZ": 0}[kind]
                    wait(pe, u_ready, t, n + 1)
                    bank, filled = mamba_fill(pe, t, f"{kind}{n}")
                    mm(bank[:, :], winC[:, k * P:(k + 1) * P], u[:, half]).then_inc(filled, 1)
                elif kind == "Dt":
                    wait(pe, u_ready, t, 2)
                    bank, filled = mamba_fill(pe, t, "Dt")
                    for c in range(TILES):
                        last = mm(bank[:, c * HEADS:(c + 1) * HEADS], u[:, c * P:(c + 1) * P], winC[:, 3 * P:INPROJ])
                    last.then_inc(filled, 1)
                elif kind == "Decay":
                    wait(pe, dA_T_ready, t, 2)
                    bank, filled = mamba_fill(pe, t, f"Decay{n}")
                    for c in range(4):
                        last = mm(bank[:, c * P:(c + 1) * P], pick_head[:, 4 * n + c, :], dA_T[:, :])
                    last.then_inc(filled, 1)
                elif kind == "XsT":
                    wait(pe, xs_ready, t)
                    bank, filled = mamba_fill(pe, t, f"XsT{n}")
                    for cols, tile in tiles_of(n):
                        last = T.transpose(bank[:, cols], xs[:, tile], ident[:, :])
                    last.then_inc(filled, 1)
                elif kind == "BT":
                    wait(pe, bc_ready, t, 2)
                    bank, filled = mamba_fill(pe, t, "BT", pe_passed)
                    for c in range(TILES):
                        last = T.transpose(bank[:, c * STATE:(c + 1) * STATE], B[:, c * P:(c + 1) * P],
                                           ident[0:STATE, 0:STATE])
                    last.then_inc(filled, 1)
                elif kind == "L":
                    wait(pe, dA_T_ready, t, 2)
                    bank, filled = mamba_fill(pe, t, f"L{n}")
                    for h in range(HEADS):
                        last = mm(bank[:, h * P:(h + 1) * P], pick(HEADS * n + h), dA_Tz[:, :])
                    last.then_inc(filled, 1)
                elif kind == "G":
                    wait(pe, bc_ready, t, 2)
                    bank, filled = mamba_fill(pe, t, f"G{n}")
                    for cols, tile in tiles_of(n):
                        last = mm(bank[:, cols], B[:, tile], C[:, tile])
                    last.then_inc(filled, 1)
                elif kind == "U":
                    wait(pe, xend_ready, t)
                    wait(pe, BT_ready, t)
                    bank, filled = mamba_fill(pe, t, "U")
                    for c in range(TILES):
                        last = mm(bank[:, c * STATE:(c + 1) * STATE],
                                  xend[:, 4 * c:4 * c + 4, :].rearrange("p a b -> p (a b)"), BT[:, c, :])
                    last.then_inc(filled, 1)
                elif kind == "StT":
                    wait(pe, state_ready, t, 3 if n == 0 else TILES - 1)
                    bank, filled = mamba_fill(pe, t, f"StT{n}", pe_passed)
                    for c in range(1 if n == 0 else 0, 4):
                        last = T.transpose(bank[0:STATE, c * P:(c + 1) * P], state[:, 4 * n + c, :], ident[:, :])
                    last.then_inc(filled, 1)
                elif kind == "Yo":
                    wait(pe, stateT_ready, t, n + 1)
                    bank, filled = mamba_fill(pe, t, f"Yo{n}")
                    for cols, tile in tiles_of(n)[1 if n == 0 else 0:]:
                        last = mm(bank[:, cols], stateT[:, tile.start // P, :], C[:, tile])
                    last.then_inc(filled, 1)
                elif kind == "Y":
                    wait(pe, M_ready, t, 4 * n + 4)
                    bank, filled = mamba_fill(pe, t, f"Y{n}")
                    for c in range(4):
                        for h in range(HEADS):
                            r = HEADS * (4 * n + c) + h
                            last = mm(bank[h * HEADDIM:(h + 1) * HEADDIM, c * P:(c + 1) * P], xdt[:, r, :],
                                      M[:, r, :])
                    last.then_inc(filled, 1)
                elif kind == "Ss":
                    wait(pe, sq_ready, t, 2)
                    bank, filled = mamba_fill(pe, t, "Ss")
                    for c in range(TILES):
                        last = mm(bank[:, c:c + 1], sq[:, c * P:(c + 1) * P], ones[:, :])
                    last.then_inc(filled, 1)
                elif kind == "Out":
                    wait(pe, y2_ready, t, n + 1)
                    bank, filled = mamba_fill(pe, t, f"Out{n}")
                    mm(bank[:, :], woutT[:, :], y2[:, half]).then_inc(filled, 1)
                elif kind == "SeA":
                    wait(pe, pooled_ready, t, 2)
                    bank, filled = mamba_fill(pe, t, "SeA")
                    mm(bank[0:SE, 0:1], se1T[:, :], pooled[:, 0:1], True, False)
                    mm(bank[0:SE, 0:1], se1T[:, :], pooled[:, 1:2], False, True).then_inc(filled, 1)
                elif kind == "SeB":
                    wait(pe, hdn_ready, t)
                    bank, filled = mamba_fill(pe, t, "SeB")
                    mm(bank[:, 0:1], se2T[:, :], hdn[:, :]).then_inc(filled, 1)

            run_streams(pe, attention, mamba, prepare)


INPUTS = ["x", "L0_conv_gn_w", "L0_conv_gn_b", "L0_conv_qkv_w", "L0_conv_qkv_b", "L0_conv_proj_w",
          "L0_conv_proj_b", "L1_conv_norm_g", "L1_conv_norm_b", "L1_conv_in_w", "L1_conv_conv_w",
          "L1_conv_conv_b", "L1_conv_dt_bias", "L1_conv_A_log", "L1_conv_Dp", "L1_conv_rms_w",
          "L1_conv_out_w", "L1_conv_se1_w", "L1_conv_se1_b", "L1_conv_se2_w", "L1_conv_se2_b"]


def kernel(**inputs):
    import numpy as np
    import concourse.bacc as bacc
    from concourse.bass_utils import run_bass_kernel_spmd

    nc = bacc.Bacc("TRN2", target_bir_lowering=False, num_devices=1)
    arrays, args = {}, []
    for name in INPUTS:
        a = np.ascontiguousarray(inputs[name])
        arrays[f"in_{name}"] = a
        args.append(nc.dram_tensor(f"in_{name}", a.shape, mybir.dt.from_np(a.dtype), kind="ExternalInput").ap())
    shape = arrays["in_x"].shape
    out = nc.dram_tensor("out", shape, F32, kind="ExternalOutput").ap()
    build(nc, *args, out)
    r = run_bass_kernel_spmd(nc, [arrays], core_ids=[0])
    return r.results[0]["out"]
```
